# Optimizing a Trainium2 kernel written in Bass

```python
import numpy as np
import jax
import jax.numpy as jnp

def _softmax(x, axis=-1):
    return jax.nn.softmax(x, axis=axis)

def _gelu(x):
    return jax.nn.gelu(x, approximate=True)

def _silu(x):
    return jax.nn.silu(x)

def _sigmoid(x):
    return jax.nn.sigmoid(x)

def _layernorm(x, axis=-1, eps=1e-05):
    m = jnp.mean(x, axis=axis, keepdims=True)
    v = jnp.var(x, axis=axis, keepdims=True)
    return (x - m) / jnp.sqrt(v + eps)

def _scatter_add(tgt, idx, src, axis=0):
    return tgt.at[idx].add(src)

def _segment_sum(src, seg, n):
    return jax.ops.segment_sum(src, seg, n)
kernel_name = 'mk_gnn_ffn_d1_gnn_r8_4e9784'

def setup_inputs(seed: int=0):
    np.random.seed(seed)
    _w = jnp.asarray

    def _rec_inputs():
        import jax
        import jax.numpy as jnp
        _gk = jax.random.key(seed)
        x = -8.776e-05 + 1 * jax.random.normal(jax.random.fold_in(_gk, 1), (2500, 256), jnp.float32)
        _s = jax.random.randint(jax.random.fold_in(_gk, 2), (20000,), 0, 2500, jnp.int32)
        _d = jax.random.randint(jax.random.fold_in(_gk, 3), (20000,), 0, 2500, jnp.int32)
        _loop = jnp.arange(2500, dtype=jnp.int32)
        src = jnp.concatenate([_s, _d, _loop])
        dst = jnp.concatenate([_d, _s, _loop])
        _o = jnp.argsort(dst, stable=True)
        src = src[_o]
        dst = dst[_o]
        edge_type_8 = jax.random.randint(jax.random.fold_in(_gk, 12), (42500,), 0, 8, jnp.int32)
        return (x, src, dst, edge_type_8)
    x, src, dst, edge_type_8 = _rec_inputs()

    def _L0_gnn_setup():
        import jax, jax.numpy as jnp
        import numpy as np
        N_NODES = 2500
        N_EDGES = 40000
        D = 256
        R = 8

        def _xavier(key, shape):
            fan_in, fan_out = (shape[-2], shape[-1])
            bound = float(np.sqrt(6.0 / (fan_in + fan_out)))
            return jax.random.uniform(key, shape, jnp.float32, -bound, bound)

        def _rgcn_layer(x, W, self_w, b, src, dst, edge_type, num_nodes):
            xW = jnp.einsum('ni,rio->rno', x, W)
            msg = xW[edge_type, src]
            agg = jax.ops.segment_sum(msg, dst, num_segments=num_nodes)
            return agg + x @ self_w + b
        key = jax.random.key(seed)
        ks = jax.random.split(key, 10)
        x = jax.random.normal(ks[0], (N_NODES, D), jnp.float32)
        edge_index = jax.random.randint(ks[1], (2, N_EDGES), 0, N_NODES)
        edge_type = jax.random.randint(ks[2], (N_EDGES,), 0, R)
        W1 = _xavier(ks[3], (R, D, D))
        self_w1 = _xavier(ks[4], (D, D))
        b1 = jnp.zeros((D,), jnp.float32)
        W2 = _xavier(ks[5], (R, D, D))
        self_w2 = _xavier(ks[6], (D, D))
        b2 = jnp.zeros((D,), jnp.float32)
        return {'x': x, 'W1': W1, 'self_w1': self_w1, 'b1': b1, 'W2': W2, 'self_w2': self_w2, 'b2': b2, 'edge_index': edge_index, 'edge_type': edge_type}
    _L0_gnn_all = _L0_gnn_setup()
    _L0_gnn_in = {k: v for k, v in _L0_gnn_all.items() if k in ('W1', 'self_w1', 'b1', 'W2', 'self_w2', 'b2')}
    del _L0_gnn_all

    def _L0_ffn_setup():
        import math
        import jax, jax.numpy as jnp
        import numpy as np
        CAPACITY_FACTOR = 1.25
        TOP_K = 2
        LN_EPS = 1e-05

        def _layer_norm(x, gamma, beta):
            mu = jnp.mean(x, axis=-1, keepdims=True)
            var = jnp.var(x, axis=-1, keepdims=True)
            return (x - mu) * jax.lax.rsqrt(var + LN_EPS) * gamma + beta
        key = jax.random.key(seed)
        ks = jax.random.split(key, 4)
        B, S, D, F, E = (8, 512, 256, 512, 8)
        x = jax.random.normal(ks[0], (B, S, D), dtype=jnp.float32)
        Wr = jax.random.normal(ks[1], (D, E), dtype=jnp.float32) / np.sqrt(D)
        br = jnp.zeros((E,), jnp.float32)
        W1 = jax.random.normal(ks[2], (E, D, F), dtype=jnp.float32) / np.sqrt(D)
        b1 = jnp.zeros((E, F), jnp.float32)
        W2 = jax.random.normal(ks[3], (E, F, D), dtype=jnp.float32) / np.sqrt(F)
        b2 = jnp.zeros((E, D), jnp.float32)
        gamma = jnp.ones((D,), jnp.float32)
        beta = jnp.zeros((D,), jnp.float32)
        return {'x': x, 'Wr': Wr, 'br': br, 'W1': W1, 'b1': b1, 'W2': W2, 'b2': b2, 'gamma': gamma, 'beta': beta}
    _L0_ffn_all = _L0_ffn_setup()
    _L0_ffn_in = {k: v for k, v in _L0_ffn_all.items() if k in ('Wr', 'br', 'W1', 'b1', 'W2', 'b2', 'gamma', 'beta')}
    del _L0_ffn_all
    return {'x': x, 'src': src, 'dst': dst, 'edge_type_8': edge_type_8, 'L0_gnn_W1': _L0_gnn_in['W1'], 'L0_gnn_self_w1': _L0_gnn_in['self_w1'], 'L0_gnn_b1': _L0_gnn_in['b1'], 'L0_gnn_W2': _L0_gnn_in['W2'], 'L0_gnn_self_w2': _L0_gnn_in['self_w2'], 'L0_gnn_b2': _L0_gnn_in['b2'], 'L0_ffn_Wr': _L0_ffn_in['Wr'], 'L0_ffn_br': _L0_ffn_in['br'], 'L0_ffn_W1': _L0_ffn_in['W1'], 'L0_ffn_b1': _L0_ffn_in['b1'], 'L0_ffn_W2': _L0_ffn_in['W2'], 'L0_ffn_b2': _L0_ffn_in['b2'], 'L0_ffn_gamma': _L0_ffn_in['gamma'], 'L0_ffn_beta': _L0_ffn_in['beta']}

def reference(x, src, dst, edge_type_8, L0_gnn_W1, L0_gnn_self_w1, L0_gnn_b1, L0_gnn_W2, L0_gnn_self_w2, L0_gnn_b2, L0_ffn_Wr, L0_ffn_br, L0_ffn_W1, L0_ffn_b1, L0_ffn_W2, L0_ffn_b2, L0_ffn_gamma, L0_ffn_beta):
    import jax
    import jax.numpy as jnp

    def _L0_gnn_ref(x, W1, self_w1, b1, W2, self_w2, b2, edge_index, edge_type):
        import jax, jax.numpy as jnp
        import numpy as np
        N_NODES = 2500
        N_EDGES = 40000
        D = 256
        R = 8

        def _xavier(key, shape):
            fan_in, fan_out = (shape[-2], shape[-1])
            bound = float(np.sqrt(6.0 / (fan_in + fan_out)))
            return jax.random.uniform(key, shape, jnp.float32, -bound, bound)

        def _rgcn_layer(x, W, self_w, b, src, dst, edge_type, num_nodes):
            xW = jnp.einsum('ni,rio->rno', x, W)
            msg = xW[edge_type, src]
            agg = jax.ops.segment_sum(msg, dst, num_segments=num_nodes)
            return agg + x @ self_w + b
        src, dst = (edge_index[0], edge_index[1])
        h = _rgcn_layer(x, W1, self_w1, b1, src, dst, edge_type, N_NODES)
        h = jax.nn.relu(h)
        out = _rgcn_layer(h, W2, self_w2, b2, src, dst, edge_type, N_NODES)
        return out

    def _L0_ffn_ref(x, Wr, br, W1, b1, W2, b2, gamma, beta):
        import math
        import jax, jax.numpy as jnp
        import numpy as np
        CAPACITY_FACTOR = 1.25
        TOP_K = 2
        LN_EPS = 1e-05

        def _layer_norm(x, gamma, beta):
            mu = jnp.mean(x, axis=-1, keepdims=True)
            var = jnp.var(x, axis=-1, keepdims=True)
            return (x - mu) * jax.lax.rsqrt(var + LN_EPS) * gamma + beta
        B, S, D = x.shape
        E = Wr.shape[1]
        N = B * S
        K = TOP_K
        logits = jnp.mean(x, axis=1) @ Wr + br
        routing_weights = jax.nn.softmax(logits, axis=-1)
        capacity = float(math.ceil(N * CAPACITY_FACTOR / E))
        expected_loads = routing_weights.sum(axis=0) * (N / B)
        scale = jnp.where(expected_loads > capacity, capacity / expected_loads, 1.0)
        routing_weights = jax.nn.softmax(routing_weights * scale, axis=-1)
        rw_tok = jnp.broadcast_to(routing_weights[:, None, :], (B, S, E)).reshape(N, E)
        top_w, top_i = jax.lax.top_k(rw_tok, K)
        top_w = jax.nn.softmax(top_w, axis=-1)
        xf = x.reshape(N, D)
        h = jax.nn.gelu(jnp.einsum('nd,edf->enf', xf, W1) + b1[:, None, :], approximate=False)
        y = jnp.einsum('enf,efd->end', h, W2) + b2[:, None, :]
        w_dense = jnp.zeros((N, E), x.dtype).at[jnp.arange(N)[:, None], top_i].add(top_w)
        out = jnp.einsum('ne,end->nd', w_dense, y).reshape(B, S, D)
        out = _layer_norm(out + x, gamma, beta)
        return out
    edge_index = jnp.stack([src, dst])
    x = x + _L0_gnn_ref(_layernorm(x, axis=-1), L0_gnn_W1, L0_gnn_self_w1, L0_gnn_b1, L0_gnn_W2, L0_gnn_self_w2, L0_gnn_b2, edge_index, edge_type_8)
    x = x + _L0_ffn_ref(_layernorm(x, axis=-1)[None], L0_ffn_Wr, L0_ffn_br, L0_ffn_W1, L0_ffn_b1, L0_ffn_W2, L0_ffn_b2, L0_ffn_gamma, L0_ffn_beta)[0]
    return x

_drawn_inputs = setup_inputs


def setup_inputs(seed=0):
    import zlib

    import numpy as np

    out = dict(_drawn_inputs(seed))
    spreads = {'L0_gnn_b1': (0.0, 0.1),
     'L0_gnn_b2': (0.0, 0.8),
     'L0_ffn_br': (0.0, 0.344),
     'L0_ffn_b1': (0.0, 0.8),
     'L0_ffn_b2': (0.0, 0.8),
     'L0_ffn_gamma': (1.0, 0.6),
     'L0_ffn_beta': (0.0, 0.8)}
    factors = {'L0_ffn_Wr': 3.383}
    for name, (base, spread) in spreads.items():
        noise = np.random.default_rng([zlib.crc32(name.encode()), seed]).standard_normal(out[name].shape)
        drawn = base * np.exp(spread * noise) if base else spread * noise
        out[name] = jnp.asarray(drawn.astype(out[name].dtype))
    for name, factor in factors.items():
        out[name] = (out[name] * factor).astype(out[name].dtype)
    return out
```

```python
from contextlib import ExitStack

import numpy as np

import concourse.bass as bass
from concourse import mybir

F32 = mybir.dt.float32
I32 = mybir.dt.int32
U32 = mybir.dt.uint32
ALU = mybir.AluOpType
ACT = mybir.ActivationFunctionType
AX = mybir.AxisListType
DVE_ENGINE = mybir.EngineType.DVE

P = 128
N, D, R, E = 2500, 256, 8, 42500
F, NE = 512, 8
LN_EPS = 1e-5
CAPACITY = float(-(-N * 5 // (4 * NE)))

EC = 128
NCH = -(-E // EC)
CFULL = E // EC
CLAST = E - CFULL * EC
ROWS = -(-NCH // P)
CTAIL = NCH - (ROWS - 1) * P
TN = 120
NT = -(-N // TN)
TLAST = N - (NT - 1) * TN
NPAD = NT * TN
WIN = 16
GC = 16
NG = NCH // GC
CREST = NCH - NG * GC
LEAD = 5
GR = 8
SR = 4
NHALF = 2 * NG + 2
PASSES = -(-N // WIN)
BASE_MAX = NPAD - WIN
MM_CREDIT = 16
ADD_CREDIT = SR
INVALID = 65536.0
RSQRT_MAGIC = float(0x5F3759DF)
KT = D // P
FT = F // P
FG = 4 * TN
FGROUPS = N // FG


def ready_chunks(t):
    return min(GC * (t + 1) + LEAD, NCH) if isinstance(t, int) else GC * (t + 1) + LEAD


def slot_uses(slot):
    return (NCH - slot + GR - 1) // GR


def program(nc, x, src, dst, etype, gW, gS, gB, Wr, br, W1, b1, W2, b2, gamma, beta, out):
    lnx = nc.dram_tensor("lnx", [N, D], F32, kind="Internal").ap()
    h1 = nc.dram_tensor("h1", [N, D], F32, kind="Internal").ap()
    table = [lnx, h1]

    ctx = ExitStack()
    with ctx:
        def sb(name, shape, dt=F32):
            return ctx.enter_context(nc.sbuf_tensor(name, shape, dt))

        def sem(name):
            return ctx.enter_context(nc.semaphore(name))

        agg = sb("agg", [P, KT, R, NPAD])
        bulk = sb("bulk", [P, NT, D])
        W = bulk[:, 0:KT * (R + 1), :]
        hout = bulk[:, 18, :]
        resid = bulk[:, 19, :]
        selfrow = bulk[:, 20, :]
        ring = sb("ring", [P, GR * D + SR * P])
        gath = [ring[:, i * D:(i + 1) * D] for i in range(GR)]
        onehot = [ring[:, GR * D + i * P:GR * D + (i + 1) * P] for i in range(SR)]
        edge_i = ring[:, 0:3 * ROWS * P].bitcast(I32).rearrange("p (a j e) -> p a j e", a=3, j=ROWS)
        edge_f = agg[:, 1, 0:1, 0:3 * ROWS * P].rearrange("p r (a j e) -> p (r a) j e", a=3, j=ROWS)
        stage = sb("stage", [P, KT * R, TN])
        selfT = sb("selfT", [P, KT, TN])
        keyT = sb("keyT", [P, NCH])
        idx = sb("idx", [P, NCH], I32)
        idx_slot = sb("idx_slot", [P, 2 * GR], I32)
        base_row = sb("base_row", [1, ROWS * P], I32)
        base_keep = sb("base_keep", [1, ROWS * P], I32)
        ident = sb("ident", [P, P])
        pattern = sb("pattern", [P, P])
        pattern_i = sb("pattern_i", [P, P], I32)
        ones = sb("ones", [1, P])
        gbias = sb("gbias", [1, D])
        small = sb("small", [P, 128])
        colsum = sb("colsum", [P, KT, NT])

        pchunk = [ctx.enter_context(nc.psum_tensor(f"pchunk{i}", [P, 512], F32)) for i in range(SR)]
        plin = ctx.enter_context(nc.psum_tensor("plin", [P, 512], F32))
        ptr = ctx.enter_context(nc.psum_tensor("ptr", [P, 512], F32))
        pxf = ctx.enter_context(nc.psum_tensor("pxf", [P, 512], F32))
        pmisc = ctx.enter_context(nc.psum_tensor("pmisc", [P, 512], F32))

        edges_in = sem("edges_in")
        x_in = [sem(f"x_in{i}") for i in range(3)]
        consts = sem("consts")
        consts_v = sem("consts_v")
        edge_clear = sem("edge_clear")
        clear = sem("clear")
        pro = sem("pro")
        rows_ready = sem("rows_ready")
        rows_turned = sem("rows_turned")
        turned_out = sem("turned_out")
        edges_ready = sem("edges_ready")
        ln_ready = sem("ln_ready")
        lnx_out = sem("lnx_out")
        w_in = sem("w_in")
        idx_ready = sem("idx_ready")
        gathered = [sem(f"gathered{i}") for i in range(GR)]
        onehot_ready = sem("onehot_ready")
        chunk_mm = sem("chunk_mm")
        chunk_add = sem("chunk_add")
        self_in = sem("self_in")
        self_turned = sem("self_turned")
        selfT_ready = sem("selfT_ready")
        staged = sem("staged")
        lin_done = sem("lin_done")
        h_ready = sem("h_ready")
        h_out = sem("h_out")
        resid_in = sem("resid_in")
        x1_ready = sem("x1_ready")
        tail = sem("tail")
        xf_ready = sem("xf_ready")
        xf_turned = sem("xf_turned")
        xfT_ready = sem("xfT_ready")
        gen_idx = sem("gen_idx")
        gen_in = sem("gen_in")
        gen_hot = sem("gen_hot")
        gen_mm = sem("gen_mm")
        gen_add = sem("gen_add")
        gen_pass = sem("gen_pass")
        route = sem("route")
        route_pe = sem("route_pe")
        route_act = sem("route_act")
        ffn_const_in = sem("ffn_const_in")
        expert_in = sem("expert_in")
        w2_ready = sem("w2_ready")
        b1_turned = sem("b1_turned")
        b1_ready = sem("b1_ready")
        up_done = sem("up_done")
        gelu_done = sem("gelu_done")
        down_done = sem("down_done")
        y_read = sem("y_read")
        fin = sem("fin")
        o_ready = sem("o_ready")
        o_out = [sem(f"o_out{i}") for i in range(2)]

        passed = sem("passed")
        passed_v = sem("passed_v")

        stats = small[:, 0:6]
        mv = small[:, 6:8]
        rs = small[:, 8:9]
        rs_var = small[:, 9:10]
        rs_tmp = small[:, 10:11]
        emin = small[:, 12:12 + ROWS]
        emax = small[:, 16:16 + ROWS]
        echk = small[:, 20:20 + ROWS]
        ebound = small[:, 24:24 + ROWS]
        ebound_i = small[:, 28:28 + ROWS].bitcast(I32)
        emaxi = small[:, 32:33]
        order_bad = small[0:1, 33:34].bitcast(I32)
        mean = small[:, 36:36 + KT]
        wcol = small[:, 40:42]
        b1T = small[:, 48:48 + 2 * FT]
        lg = small[0:1, 56:64]
        ex = small[0:1, 64:72]
        top = small[0:1, 72:80]
        top_i = small[0:1, 80:88].bitcast(U32)
        r1 = small[0:1, 88:89]
        r2 = small[0:1, 89:90]
        zero = small[:, 126:127].rearrange("p (a b) -> p a b", a=1)
        brow = small[0:1, 96:104]
        sumc = small[:, 104:104 + KT]
        WrT = small[:, 108:108 + KT * NE].rearrange("p (k e) -> p k e", k=KT)

        def x1_view(t, m):
            return agg[0:m, 0, 0:4, bass.ds(TN * t, 64)]

        def xf_view(t, m):
            return agg[0:m, 0, 4:8, bass.ds(TN * t, 64)]

        xfT = agg[:, 1, 0:KT, :]
        late = agg[:, 1, KT:R, :].rearrange("p r n -> p (r n)")
        at = 0

        def carve(cols):
            nonlocal at
            at += cols
            assert at <= (R - KT) * NPAD
            return late[:, at - cols:at]
        w1e = carve(2 * KT * F).rearrange("p (e k f) -> p e k f", e=2, k=KT)
        w2e = carve(2 * FT * D).rearrange("p (e k d) -> p e k d", e=2, k=FT)
        hid = carve(2 * FT * FG).rearrange("p (k n) -> p k n", k=2 * FT)
        gam = carve(D)
        bet = carve(D)
        b1rows = carve(P)
        b2rows = carve(2 * D).rearrange("p (e d) -> p e d", e=2)
        b2w = carve(D)
        zrow = [carve(D), carve(D)]

        ln_stats = keyT[:, 0:6 * NT].rearrange("p (t s) -> p t s", s=6)
        ln_mv = keyT[:, 6 * NT:8 * NT].rearrange("p (t s) -> p t s", s=2)
        ln_rs = keyT[:, 8 * NT:9 * NT]
        ln_var = keyT[:, 9 * NT:10 * NT]
        ln_tmp = keyT[:, 10 * NT:11 * NT]

        block = ctx.enter_context(nc.Block())

        def rsqrt_steps(eng, step, y, v, var, tmp):
            yi, vi = y.bitcast(I32), v.bitcast(I32)
            step(eng.tensor_scalar(v, var, LN_EPS, None, ALU.add))
            step(eng.tensor_scalar(yi, vi, 1, None, ALU.arith_shift_right))
            step(eng.tensor_scalar(yi, yi, -1.0, RSQRT_MAGIC, ALU.mult, ALU.add))
            for _ in range(3):
                step(eng.tensor_tensor(tmp, y, y, ALU.mult))
                step(eng.tensor_tensor(tmp, tmp, v, ALU.mult))
                step(eng.tensor_scalar(tmp, tmp, -0.5, 1.5, ALU.mult, ALU.add))
                step(eng.tensor_tensor(y, y, tmp, ALU.mult))
        RSQRT_N = 15

        XB = [(0, 7), (7, 14), (14, NT)]

        @block.sync
        def _(eng):
            lists = (dst, etype, src)
            for a, lst in enumerate(lists):
                full = (ROWS - 1) * P * EC
                eng.dma_start(edge_i[:, a, 0:ROWS - 1, :],
                              lst[0:full].rearrange("(j p e) -> p j e", p=P, e=EC)).then_inc(edges_in, 16)
            eng.wait_ge(edge_clear, 1)
            for a, lst in enumerate(lists):
                full = (ROWS - 1) * P * EC
                eng.dma_start(edge_i[0:CTAIL - 1, a, ROWS - 1, :],
                              lst[full:CFULL * EC].rearrange("(p e) -> p e", e=EC)).then_inc(edges_in, 16)
                if a == 0:
                    eng.dma_start(edge_i[CTAIL - 1:CTAIL, a, ROWS - 1, :],
                                  lst[E - EC:E].rearrange("(p e) -> p e", p=1)).then_inc(edges_in, 16)
                else:
                    eng.dma_start(edge_i[CTAIL - 1:CTAIL, a, ROWS - 1, EC - CLAST:EC],
                                  lst[E - CLAST:E].rearrange("(p e) -> p e", p=1)).then_inc(edges_in, 16)
            eng.dma_start(WrT, Wr.rearrange("(k p) e -> p k e", p=P)).then_inc(ffn_const_in, 16)
            eng.dma_start(brow, br.rearrange("(a e) -> a e", a=1)).then_inc(ffn_const_in, 16)
            for b, (t0, t1) in enumerate(XB):
                eng.wait_ge(ln_ready, b + 1)
                tf = min(t1, NT - 1)
                eng.dma_start(lnx[t0 * TN:tf * TN, :].rearrange("(t p) d -> p t d", p=TN),
                              bulk[0:TN, t0:tf, :]).then_inc(lnx_out, 16)
            eng.dma_start(lnx[(NT - 1) * TN:N, :], bulk[0:TLAST, NT - 1, :]).then_inc(lnx_out, 16)

            def load_weights(L):
                eng.dma_start(W[:, 0:KT * R, :], gW[L].rearrange("r (h p) o -> p (r h) o", p=P)).then_inc(w_in, 16)
                eng.dma_start(W[:, KT * R:, :], gS[L].rearrange("(h p) o -> p h o", p=P)).then_inc(w_in, 16)
                eng.dma_start(gbias[:, :], gB[L].rearrange("(a d) -> a d", a=1)).then_inc(w_in, 16)

            def load_rows(L, t, m):
                T = L * NT + t
                eng.wait_ge(self_turned, T + 1)
                eng.dma_start(selfrow[0:m, :], table[L][bass.ds(TN * t, m), :]).then_inc(self_in, 16)
                if L == 1:
                    eng.wait_ge(x1_ready, t + 1)
                    eng.dma_start(resid[0:m, :], x[bass.ds(TN * t, m), :]).then_inc(resid_in, 16)

            def store_h(t, m):
                eng.wait_ge(h_ready, t + 2)
                eng.dma_start(h1[bass.ds(TN * t, m), :], hout[0:m, :]).then_inc(h_out, 16)

            for L in range(2):
                if L == 0:
                    eng.wait_ge(lnx_out, 64)
                else:
                    eng.wait_ge(h_out, 16 * NT + 16)
                    eng.wait_ge(lin_done, NT + 1)
                load_weights(L)
                with eng.Fori(0, NT - 1) as t:
                    load_rows(L, t, TN)
                    if L == 0:
                        store_h(t, TN)
                load_rows(L, NT - 1, TLAST)
                if L == 0:
                    store_h(NT - 1, TLAST)
            eng.wait_ge(lin_done, 2 * NT + 1)
            eng.dma_start(gam, gamma.rearrange("(a d) -> a d", a=1).to_broadcast([P, D])).then_inc(ffn_const_in, 16)
            eng.dma_start(bet, beta.rearrange("(a d) -> a d", a=1).to_broadcast([P, D])).then_inc(ffn_const_in, 16)
            eng.wait_ge(route, ROUTE_TOP)
            for k in range(2):
                e = eng.value_load(top_i[0:1, k:k + 1], min_val=0, max_val=NE - 1)
                eng.dma_start(w1e[:, k, :, :],
                              W1[bass.ds(e, 1), :, :].rearrange("a (k p) f -> p (a k) f", p=P)).then_inc(expert_in, 16)
                eng.dma_start(b1rows[FT * k:FT * (k + 1), :],
                              b1[bass.ds(e, 1), :].rearrange("a (k p) -> (a k) p", p=P)).then_inc(expert_in, 16)
                eng.dma_start(b2rows[0:1, k, :], b2[bass.ds(e, 1), :]).then_inc(expert_in, 16)
                eng.dma_start(w2e[:, k, :, :],
                              W2[bass.ds(e, 1), :, :].rearrange("a (k p) d -> p (a k) d", p=P)).then_inc(expert_in, 16)
            with eng.Fori(0, (NT - 1) // 2) as u:
                for i in range(2):
                    eng.wait_ge(o_ready, 2 * u + i + 1)
                    eng.dma_start(out[bass.ds(TN * (2 * u + i), TN), :], zrow[i][0:TN, :]).then_inc(o_out[i], 16)
            eng.wait_ge(o_ready, NT)
            eng.dma_start(out[(NT - 1) * TN:N, :], zrow[0][0:TLAST, :]).then_inc(o_out[0], 16)
            eng.wait_ge(o_out[0], 16 * ((NT - 1) // 2 + 1) + 16)
            eng.wait_ge(o_out[1], 16 * ((NT - 1) // 2) + 16)

        @block.gpsimd
        def _(eng):
            eng.memset(ident[:, :], 0.0).then_inc(consts, 1)
            eng.iota(pattern_i[:, :], pattern=[[1, R], [R, WIN]], base=0, channel_multiplier=0).then_inc(consts, 1)
            eng.iota(ebound_i[:, :], pattern=[[P, ROWS]], base=-LEAD, channel_multiplier=1).then_inc(consts, 1)
            eng.wait_ge(consts, 1)
            eng.affine_select(out=ident[:, :], in_=ident[:, :], compare_op=ALU.not_equal, fill=1.0,
                              base=0, pattern=[[-1, P]], channel_multiplier=1).then_inc(consts, 1)
            eng.memset(agg[:, 0, :, :], 0.0).then_inc(clear, 1)
            eng.wait_ge(edges_ready, 1)
            bad = eng.value_load(order_bad, min_val=0, max_val=1)
            with eng.If(bad == 0):
                for L in range(2):
                    def gather(g, j):
                        s = j % GR
                        eng.wait_ge(idx_ready, L * NHALF + 2 * g + j // GR + 1)
                        eng.wait_ge(chunk_mm, MM_CREDIT + L * NCH + GC * g + j - GR + 1)
                        eng.sem_inc(passed, 1)
                        eng.indirect_dma_start(out=gath[s], out_offset=None, in_=table[L][:, :],
                                               in_offset=bass.IndirectOffsetOnAxis(
                                                   ap=idx_slot[:, j:j + 1], axis=0)).then_inc(gathered[s], 16)
                    if L == 0:
                        eng.wait_ge(lnx_out, 64)
                    else:
                        eng.wait_ge(h_out, 16 * NT + 16)
                    with eng.Fori(0, NG) as g:
                        for j in range(GC):
                            gather(g, j)
                    for j in range(CREST):
                        gather(NG, j)
            with eng.Else():
                for L in range(2):
                    if L == 0:
                        eng.wait_ge(lnx_out, 64)
                    else:
                        eng.wait_ge(h_out, 16 * NT + 16)
                    with eng.Fori(0, PASSES) as k:
                        with eng.Fori(0, NCH) as c:
                            n = (L * PASSES + k) * NCH + c
                            eng.wait_ge(gen_mm, n + 1)
                            eng.tensor_copy(idx_slot[:, 0:1], idx[:, bass.ds(c, 1)]).then_inc(gen_idx, 1)
                            eng.wait_ge(gen_idx, n + 1)
                            eng.sem_inc(passed, 1)
                            eng.indirect_dma_start(out=gath[0], out_offset=None, in_=table[L][:, :],
                                                   in_offset=bass.IndirectOffsetOnAxis(
                                                       ap=idx_slot[:, 0:1], axis=0)).then_inc(gen_in, 16)

        @block.scalar
        def _(eng):
            for b, (t0, t1) in enumerate(XB):
                tf = min(t1, NT - 1)
                eng.dma_start(bulk[0:TN, t0:tf, :],
                              x[t0 * TN:tf * TN, :].rearrange("(t p) d -> p t d", p=TN)).then_inc(x_in[b], 16)
            eng.dma_start(bulk[0:TLAST, NT - 1, :], x[(NT - 1) * TN:N, :]).then_inc(x_in[2], 16)

            def turn_self(L, t, m):
                T = L * NT + t
                eng.wait_ge(self_turned, T + 2)
                eng.wait_ge(lin_done, T + 1)
                eng.activation(selfT[:, :, 0:m], ptr[:, 0:KT * m].rearrange("p (k n) -> p k n", k=KT),
                               ACT.Copy).then_inc(selfT_ready, 1)

            def stage_tile(L, t, m):
                T = L * NT + t
                eng.wait_ge(lin_done, T + 1)
                eng.activation(stage[:, :, 0:m],
                               agg[:, :, :, bass.ds(TN * t, m)].rearrange("p h r n -> p (h r) n"),
                               ACT.Copy).then_inc(staged, 1)

            def relu_rows(t, m):
                eng.wait_ge(lin_done, t + 2)
                eng.wait_ge(h_out, 16 * t + 16)
                eng.activation(hout[0:m, :], plin[0:m, 0:D], ACT.Relu).then_inc(h_ready, 1)

            def keep_xfT(t, m):
                eng.wait_ge(xf_turned, t + 1)
                for h in range(KT):
                    ins = eng.activation(xfT[:, h, bass.ds(TN * t, m)], pxf[:, h * TN:h * TN + m], ACT.Identity,
                                         accum_out=colsum[:, h, bass.ds(t, 1)])
                ins.then_inc(xfT_ready, 1)

            def copy_indices(L, half, c0, cols):
                eng.wait_ge(chunk_mm, MM_CREDIT + L * NCH + c0 - GR)
                eng.activation(idx_slot[:, half * GR:half * GR + cols], idx[:, bass.ds(c0, cols)],
                               ACT.Copy).then_inc(idx_ready, 1)

            eng.wait_ge(edges_ready, 1)
            bad = eng.value_load(order_bad, min_val=0, max_val=1)
            with eng.If(bad == 0):
                for L in range(2):
                    def tile_work(t, m, chunks):
                        turn_self(L, t, m)
                        eng.wait_ge(chunk_add, ADD_CREDIT + L * NCH + chunks)
                        stage_tile(L, t, m)

                    def tile_end(t, m):
                        if L == 0:
                            relu_rows(t, m)
                        else:
                            keep_xfT(t, m)

                    if L == 1:
                        eng.wait_ge(chunk_mm, MM_CREDIT + NCH)
                    copy_indices(L, 0, 0, GR)
                    copy_indices(L, 1, GR, GR)
                    copy_indices(L, 0, GC, GR)
                    copy_indices(L, 1, GC + GR, GR)
                    with eng.Fori(1, NG - 1) as g:
                        tile_work(g - 1, TN, ready_chunks(g - 1))
                        copy_indices(L, 0, GC * g + GC, GR)
                        tile_end(g - 1, TN)
                        copy_indices(L, 1, GC * g + GC + GR, GR)
                    g = NG - 1
                    tile_work(g - 1, TN, ready_chunks(g - 1))
                    copy_indices(L, 0, GC * NG, GR)
                    tile_end(g - 1, TN)
                    copy_indices(L, 1, GC * NG + GR, CREST - GR)
                    tile_work(NT - 2, TN, ready_chunks(NT - 2))
                    tile_end(NT - 2, TN)
                    tile_work(NT - 1, TLAST, NCH)
                    tile_end(NT - 1, TLAST)
            with eng.Else():
                for L in range(2):
                    eng.wait_ge(gen_add, (L + 1) * PASSES * NCH + 1)

                    def tile(t, m):
                        turn_self(L, t, m)
                        stage_tile(L, t, m)
                        if L == 0:
                            relu_rows(t, m)
                        else:
                            keep_xfT(t, m)
                    with eng.Fori(0, NT - 1) as t:
                        tile(t, TN)
                    tile(NT - 1, TLAST)
            eng.wait_ge(route, ROUTE_LOGITS)
            eng.activation(ex, lg, ACT.Exp).then_inc(route_act, 1)
            eng.wait_ge(route, ROUTE_SCALED)
            eng.activation(ex, lg, ACT.Exp).then_inc(route_act, 1)
            eng.wait_ge(route, ROUTE_DIFF)
            eng.activation(ex[:, 0:2], lg[:, 0:2], ACT.Exp).then_inc(route_act, 1)
            eng.wait_ge(b1_ready, 1)

            def gelu(first, m):
                for k in range(2 * FT):
                    eng.wait_ge(up_done, first + k + 1)
                    eng.activation(hid[:, k, 0:m], pchunk[k % SR][:, 0:m], ACT.Gelu,
                                   bias=b1T[:, k:k + 1]).then_inc(gelu_done, 1)
            with eng.Fori(0, FGROUPS) as q:
                gelu(2 * FT * q, FG)
            gelu(2 * FT * FGROUPS, N - FG * FGROUPS)

        @block.tensor
        def _(eng):
            eng.wait_ge(consts, 4)
            eng.wait_ge(rows_ready, 1)
            blocks = [(a, j) for a in range(2) for j in range(ROWS)]
            for n, (a, j) in enumerate(blocks):
                m = P if j < ROWS - 1 else CTAIL
                if n >= SR:
                    eng.wait_ge(turned_out, n - SR + 1)
                eng.transpose(pchunk[n % SR][:, 0:m], edge_f[0:m, a + 1, j, :], ident[0:m, 0:m]).then_inc(rows_turned, 1)
            for j in range(ROWS):
                ins = eng.transpose(plin[0:1, j * P:(j + 1) * P], emin[:, j:j + 1], ident[:, :])
            ins.then_inc(rows_turned, 1)
            eng.transpose(ptr[0:1, 0:P], emaxi, ident[:, :]).then_inc(rows_turned, 1)
            eng.wait_ge(edges_ready, 1)
            bad = eng.value_load(order_bad, min_val=0, max_val=1)

            def turn_self(L, t, m):
                T = L * NT + t
                eng.wait_ge(self_in, 16 * T + 16)
                eng.wait_ge(selfT_ready, T + 1)
                for h in range(KT):
                    ins = eng.transpose(ptr[:, h * m:(h + 1) * m], selfrow[0:m, h * P:(h + 1) * P], ident[0:m, 0:m])
                ins.then_inc(self_turned, 1)

            def products(L, t, m, k0, k1):
                T = L * NT + t
                for k in range(k0, k1):
                    if k == 0:
                        if L == 0:
                            eng.wait_ge(h_ready, t + 1)
                        else:
                            eng.wait_ge(h_ready, NT + 1)
                            eng.wait_ge(x1_ready, t + 1)
                        eng.matmul(plin[0:m, 0:D], ones[0:1, 0:m], gbias[0:1, :], start=True, stop=False)
                    elif k <= KT:
                        if k == 1:
                            eng.wait_ge(selfT_ready, T + 2)
                        eng.matmul(plin[0:m, 0:D], selfT[:, k - 1, 0:m], W[:, KT * R + k - 1, :], start=False, stop=False)
                    else:
                        if k == KT + 1:
                            eng.wait_ge(staged, T + 1)
                        h, r = (k - KT - 1) // R, (k - KT - 1) % R
                        ins = eng.matmul(plin[0:m, 0:D], stage[:, h * R + r, 0:m], W[:, KT * r + h, :],
                                         start=False, stop=(k == KT * (R + 1)))
                        if k == KT * (R + 1):
                            ins.then_inc(lin_done, 1)
            STEPS = KT * (R + 1) + 1

            def turn_xf(t, m):
                eng.wait_ge(xf_ready, t + 1)
                eng.wait_ge(xfT_ready, t + 1)
                for h in range(KT):
                    ins = eng.transpose(pxf[:, h * TN:h * TN + m], hout[0:m, h * P:(h + 1) * P], ident[0:m, 0:m])
                ins.then_inc(xf_turned, 1)

            with eng.If(bad == 0):
                for L in range(2):
                    def chunk(g, j):
                        s = j % GR
                        first = j // GR + 1 + L * slot_uses(s)
                        eng.wait_ge(gathered[s], 16 * (2 * g + first))
                        eng.wait_ge(onehot_ready, L * NCH + GC * g + j + 1)
                        eng.wait_ge(chunk_add, L * NCH + GC * g + j + 1)
                        for h in range(KT):
                            ins = eng.matmul(pchunk[j % SR][:, h * P:(h + 1) * P], gath[s][:, h * P:(h + 1) * P],
                                             onehot[j % SR], start=True, stop=True)
                        ins.then_inc(chunk_mm, 1)

                    def group(g, chunks, tile):
                        step, left = 0, chunks - 7
                        for j in range(chunks):
                            chunk(g, j)
                            if tile is None:
                                continue
                            if j == 3:
                                turn_self(L, tile, TN)
                            if j >= 7:
                                to = -(-STEPS * (j - 6) // min(left, 7))
                                to = min(to, STEPS)
                                products(L, tile, TN, step, to)
                                step = to
                        if tile is not None:
                            products(L, tile, TN, step, STEPS)
                            if L == 1:
                                turn_xf(tile, TN)

                    eng.wait_ge(chunk_add, ADD_CREDIT + L * NCH)
                    group(0, GC, None)
                    eng.wait_ge(w_in, 48 * (L + 1))
                    with eng.Fori(1, NG) as g:
                        group(g, GC, g - 1)
                    group(NG, CREST, NT - 2)
                    turn_self(L, NT - 1, TLAST)
                    products(L, NT - 1, TLAST, 0, STEPS)
                    if L == 1:
                        turn_xf(NT - 1, TLAST)
            with eng.Else():
                for L in range(2):
                    with eng.Fori(0, PASSES) as k:
                        with eng.Fori(0, NCH) as c:
                            n = (L * PASSES + k) * NCH + c
                            eng.wait_ge(gen_in, 16 * n + 16)
                            eng.wait_ge(gen_hot, n + 1)
                            eng.wait_ge(gen_add, n + 1)
                            for h in range(KT):
                                ins = eng.matmul(pchunk[0][:, h * P:(h + 1) * P], gath[0][:, h * P:(h + 1) * P],
                                                 onehot[0], start=True, stop=True)
                            ins.then_inc(gen_mm, 1)
                    eng.wait_ge(w_in, 48 * (L + 1))

                    def tile(t, m):
                        turn_self(L, t, m)
                        products(L, t, m, 0, STEPS)
                        if L == 1:
                            turn_xf(t, m)
                    with eng.Fori(0, NT - 1) as t:
                        tile(t, TN)
                    tile(NT - 1, TLAST)
            eng.wait_ge(ffn_const_in, 64)
            eng.wait_ge(route, ROUTE_MEAN)
            for k in range(KT):
                ins = eng.matmul(pmisc[0:1, 0:NE], mean[:, k:k + 1], WrT[:, k, :], start=(k == 0), stop=(k == KT - 1))
            ins.then_inc(route_pe, 1)
            eng.wait_ge(expert_in, 16 * 8)
            eng.transpose(ptr[:, 0:2 * FT], b1rows[0:2 * FT, :], ident[0:2 * FT, 0:2 * FT]).then_inc(b1_turned, 1)
            eng.wait_ge(route, ROUTE_WEIGHTS)
            eng.matmul(pmisc[:, 0:2], ones[0:1, :], lg[:, 2:4], start=True, stop=True).then_inc(route_pe, 1)

            ybank = [plin, ptr, pxf, pmisc]

            def ffn(q, m, tiles):
                for k in range(2 * FT):
                    e, f = k // FT, k % FT
                    eng.wait_ge(gelu_done, 2 * FT * q + k + 1)
                    for i in range(KT):
                        ins = eng.matmul(pchunk[k % SR][:, 0:m], w1e[:, e, i, f * P:(f + 1) * P],
                                         xfT[:, i, bass.ds(FG * q, m)], start=(i == 0), stop=(i == KT - 1))
                    ins.then_inc(up_done, 1)
                for i, mt in enumerate(tiles):
                    eng.wait_ge(y_read, 4 * q + i + 1)
                    if i == 0:
                        eng.wait_ge(w2_ready, 1)
                    eng.matmul(ybank[i][0:mt, 0:D], ones[0:1, 0:mt], b2w[0:1, :], start=True, stop=False)
                    for k in range(2 * FT):
                        if i == 0:
                            eng.wait_ge(gelu_done, SR + 2 * FT * q + k + 1)
                        ins = eng.matmul(ybank[i][0:mt, 0:D], hid[:, k, i * TN:i * TN + mt],
                                         w2e[:, k // FT, k % FT, :], start=False, stop=(k == 2 * FT - 1))
                    ins.then_inc(down_done, 1)
            eng.wait_ge(xfT_ready, NT + 1)
            with eng.Fori(0, FGROUPS) as q:
                ffn(q, FG, [TN] * 4)
            ffn(FGROUPS, TLAST, [TLAST])

        @block.vector
        def _(eng):
            eng.sem_inc(chunk_mm, MM_CREDIT)
            eng.sem_inc(chunk_add, ADD_CREDIT)
            for s in (self_turned, selfT_ready, lin_done, h_ready, x1_ready, xfT_ready, gen_mm, gen_add):
                eng.sem_inc(s, 1)
            for s in (h_out, o_out[0], o_out[1]):
                eng.sem_inc(s, 16)
            eng.sem_inc(gelu_done, SR)
            eng.sem_inc(y_read, 4)

            count = [0]

            def step(ins):
                count[0] += 1
                ins.then_inc(pro, 1)
                eng.wait_ge(pro, count[0])

            eng.memset(edge_i[:, 0, ROWS - 1, :], 0)
            eng.memset(edge_i[:, 2, ROWS - 1, :], 0)
            eng.memset(edge_i[:, 1, ROWS - 1, :], int(INVALID)).then_inc(edge_clear, 1)
            eng.memset(ones[:, :], 1.0).then_inc(consts_v, 1)
            eng.memset(small[:, 126:127], 0.0).then_inc(consts_v, 1)
            eng.memset(echk[:, :], -1.0).then_inc(consts_v, 1)
            eng.wait_ge(consts, 4)
            step(eng.tensor_copy(pattern[:, :], pattern_i[:, :]))

            for b, (t0, t1) in enumerate(XB):
                eng.wait_ge(x_in[b], 16 if b < 2 else 32)
                for t in range(t0, t1):
                    m = TN if t < NT - 1 else TLAST
                    ins = eng.bn_stats(ln_stats[0:m, t, :], bulk[0:m, t, :])
                step(ins)
                for t in range(t0, t1):
                    m = TN if t < NT - 1 else TLAST
                    ins = eng.bn_aggr(ln_mv[0:m, t, :], ln_stats[0:m, t, :])
                step(ins)
                for lo, hi, m in [(t0, min(t1, NT - 1), TN)] + [(NT - 1, NT, TLAST)] * (t1 == NT):
                    rsqrt_steps(eng, step, ln_rs[0:m, lo:hi], ln_var[0:m, lo:hi], ln_mv[0:m, lo:hi, 1],
                                ln_tmp[0:m, lo:hi])
                for t in range(t0, t1):
                    m = TN if t < NT - 1 else TLAST
                    ins = eng.tensor_scalar(bulk[0:m, t, :], bulk[0:m, t, :], ln_mv[0:m, t, 0:1], ln_rs[0:m, t:t + 1],
                                            ALU.subtract, ALU.mult)
                ins.then_inc(ln_ready, 1)

            eng.wait_ge(ln_ready, 3)

            eng.wait_ge(edges_in, 16 * 9)
            step(eng.tensor_copy(edge_f, edge_i))
            step(eng.tensor_reduce(emin, edge_f[:, 0, :, :], AX.X, ALU.min))
            step(eng.tensor_reduce(emax, edge_f[:, 0, :, :], AX.X, ALU.max))
            step(eng.tensor_scalar(ebound_i, ebound_i, GC.bit_length() - 1, None, ALU.arith_shift_right))
            step(eng.tensor_scalar(ebound, ebound_i, float(TN), None, ALU.mult))
            step(eng.tensor_tensor(ebound, ebound, emin, ALU.subtract))
            step(eng.tensor_tensor(emax, emax, emin, ALU.subtract))
            step(eng.tensor_scalar(emax, emax, float(WIN - 1), None, ALU.subtract))
            eng.wait_ge(consts_v, 3)
            eng.tensor_tensor(echk[:, 0:ROWS - 1], emax[:, 0:ROWS - 1], ebound[:, 0:ROWS - 1], ALU.max)
            step(eng.tensor_tensor(echk[0:CTAIL, ROWS - 1:], emax[0:CTAIL, ROWS - 1:], ebound[0:CTAIL, ROWS - 1:],
                                   ALU.max))
            step(eng.tensor_reduce(emaxi, echk, AX.X, ALU.max))
            for j in range(ROWS):
                ins = eng.tensor_scalar(edge_f[:, 0, j, :], edge_f[:, 0, j, :], emin[:, j:j + 1], float(R),
                                        ALU.subtract, ALU.mult)
            step(ins)
            eng.tensor_tensor(edge_f[:, 1, :, :], edge_f[:, 1, :, :], edge_f[:, 0, :, :],
                              ALU.add).then_inc(rows_ready, 1)
            blocks = [(a, j) for a in range(2) for j in range(ROWS)]
            for n, (a, j) in enumerate(blocks):
                m = P if j < ROWS - 1 else CTAIL
                eng.wait_ge(rows_turned, n + 1)
                to = keyT if a == 0 else idx
                ins = eng.tensor_copy(to[:, j * P:j * P + m], pchunk[n % SR][:, 0:m]).then_inc(turned_out, 1)
            eng.wait_ge(rows_turned, len(blocks) + 2)
            step(eng.tensor_copy(base_row[:, :], plin[0:1, 0:ROWS * P]))
            step(eng.tensor_copy(base_keep[:, :], plin[0:1, 0:ROWS * P]))
            step(eng.tensor_reduce(r1, ptr[0:1, 0:P], AX.X, ALU.max))
            step(eng.tensor_scalar(order_bad, r1, 0.5, None, ALU.is_gt))
            eng.wait_ge(turned_out, len(blocks))
            eng.memset(agg[:, 1, :, :], 0.0).then_inc(edges_ready, 1)
            eng.wait_ge(edges_ready, 1)
            bad = eng.value_load(order_bad, min_val=0, max_val=1)
            eng.wait_ge(clear, 1)

            def tile_tail(t, m):
                n = [TAIL_N * t]

                def step(ins):
                    n[0] = n[0] + 1
                    ins.then_inc(tail, 1)
                    eng.wait_ge(tail, n[0])
                eng.wait_ge(lin_done, NT + t + 2)
                eng.wait_ge(resid_in, 16 * t + 16)
                step(eng.tensor_tensor(resid[0:m, :], plin[0:m, 0:D], resid[0:m, :], ALU.add))
                step(eng.bn_stats(stats[0:m, :], resid[0:m, :]))
                eng.sem_inc(passed_v, 1)
                step(eng.bn_aggr(mv[0:m, :], stats[0:m, :]))
                rsqrt_steps(eng, step, rs[0:m, :], rs_var[0:m, :], mv[0:m, 1:2], rs_tmp[0:m, :])
                eng.wait_ge(xfT_ready, t + 1)
                step(eng.tensor_scalar(hout[0:m, :], resid[0:m, :], mv[0:m, 0:1], rs[0:m, :],
                                       ALU.subtract, ALU.mult))
                eng.tensor_copy(x1_view(t, m), resid[0:m, :].rearrange("p (a b) -> p a b", a=4)).then_inc(x1_ready, 1)
                eng.tensor_copy(xf_view(t, m), hout[0:m, :].rearrange("p (a b) -> p a b", a=4)).then_inc(xf_ready, 1)
            TAIL_N = 4 + RSQRT_N

            with eng.If(bad == 0):
                for L in range(2):
                    def one_hot(g, j):
                        eng.tensor_scalar(onehot[j % SR], pattern[:, :], keyT[:, bass.ds(GC * g + j, 1)], None,
                                          ALU.is_equal).then_inc(onehot_ready, 1)

                    def group(g, chunks, tile):
                        _, base = nc.values_load_multi_w_load_instructions(
                            base_row[0:1, bass.ds(GC * g, GC)], engines=[DVE_ENGINE], min_val=0, max_val=BASE_MAX,
                            skip_runtime_bounds_check_because="a destination node is below N, and a window from there "
                            "ends inside agg")
                        for j in range(chunks):
                            if chunks == GC or j + SR - 1 < chunks:
                                one_hot(g, j + SR - 1)
                            c = L * NCH + GC * g + j
                            eng.wait_ge(chunk_mm, MM_CREDIT + c + 1)
                            eng.wait_ge(chunk_add, ADD_CREDIT + c)
                            to = agg[:, :, :, bass.ds(base[j], WIN)]
                            eng.tensor_tensor(to, to, pchunk[j % SR][:, 0:KT * P].rearrange(
                                "p (h r n) -> p h r n", h=KT, r=R), ALU.add).then_inc(chunk_add, 1)
                            if L == 0 and tile is not None and j == 11:
                                clear_tile(tile)
                        if L == 1 and tile is not None:
                            tile_tail(tile, TN)

                    def clear_tile(tile):
                        eng.wait_ge(staged, tile + 1)
                        eng.tensor_scalar(agg[:, :, :, bass.ds(TN * tile, TN)].rearrange("p h r n -> p (h r) n"),
                                          zero.to_broadcast([P, KT * R, TN]), 0.0, None, ALU.add)

                    for j in range(SR - 1):
                        one_hot(0, j)
                    group(0, GC, None)
                    with eng.Fori(1, NG) as g:
                        group(g, GC, g - 1)
                    group(NG, CREST, NT - 2)
                    if L == 0:
                        clear_tile(NT - 1)
                    else:
                        tile_tail(NT - 1, TLAST)
            with eng.Else():
                for L in range(2):
                    with eng.Fori(0, PASSES) as k:
                        with eng.Fori(0, NCH) as c:
                            n = (L * PASSES + k) * NCH + c
                            base = eng.value_load(base_row[0:1, bass.ds(c, 1)], min_val=0, max_val=BASE_MAX)
                            eng.wait_ge(gen_mm, n + 1)
                            eng.tensor_scalar(onehot[0], pattern[:, :], keyT[:, bass.ds(c, 1)], None,
                                              ALU.is_equal).then_inc(gen_hot, 1)
                            eng.wait_ge(gen_mm, n + 2)
                            eng.wait_ge(gen_add, n + 1)
                            to = agg[:, :, :, bass.ds(base, WIN)]
                            eng.tensor_tensor(to, to, pchunk[0][:, 0:KT * P].rearrange(
                                "p (h r n) -> p h r n", h=KT, r=R), ALU.add).then_inc(gen_add, 1)
                        q = L * (2 * PASSES + 3) + 2 * k
                        eng.tensor_scalar(keyT[:, :], keyT[:, :], float(WIN * R), None,
                                          ALU.subtract).then_inc(gen_pass, 1)
                        eng.tensor_scalar(base_row[:, :], base_row[:, :], float(WIN), float(BASE_MAX), ALU.add,
                                          ALU.min).then_inc(gen_pass, 1)
                        eng.wait_ge(gen_pass, q + 2)
                    q = L * (2 * PASSES + 3) + 2 * PASSES
                    eng.tensor_scalar(keyT[:, :], keyT[:, :], float(WIN * R * PASSES), None,
                                      ALU.add).then_inc(gen_pass, 1)
                    eng.tensor_copy(base_row[:, :], base_keep[:, :]).then_inc(gen_pass, 1)
                    eng.wait_ge(gen_pass, q + 2)
                    if L == 0:
                        eng.wait_ge(staged, NT)
                        eng.memset(agg[:, :, :, :], 0.0).then_inc(gen_pass, 1)
                        eng.wait_ge(gen_pass, q + 3)
                    else:
                        with eng.Fori(0, NT - 1) as t:
                            tile_tail(t, TN)
                        tile_tail(NT - 1, TLAST)

            n = [0]

            def step(ins):
                n[0] += 1
                ins.then_inc(route, 1)
                eng.wait_ge(route, n[0])

            def mark(want):
                assert n[0] == want, (n[0], want)

            def soft(total):
                step(eng.tensor_reduce(r1, ex[:, 0:total], AX.X, ALU.add))
                step(eng.reciprocal(r2, r1))

            eng.wait_ge(xfT_ready, NT + 1)
            step(eng.tensor_reduce(sumc, colsum[:, :, :], AX.X, ALU.add))
            step(eng.tensor_scalar(mean, sumc, 1.0 / N, None, ALU.mult))
            mark(ROUTE_MEAN)
            eng.wait_ge(ffn_const_in, 64)
            eng.wait_ge(route_pe, 1)
            step(eng.tensor_tensor(lg, pmisc[0:1, 0:NE], brow, ALU.add))
            step(eng.tensor_reduce(r1, lg, AX.X, ALU.max))
            step(eng.tensor_scalar(lg, lg, r1, None, ALU.subtract))
            mark(ROUTE_LOGITS)
            eng.wait_ge(route_act, 1)
            soft(NE)
            step(eng.tensor_scalar(ex, ex, r2, None, ALU.mult))
            step(eng.tensor_scalar(lg, ex, float(N), 1e-30, ALU.mult, ALU.max))
            step(eng.reciprocal(lg, lg))
            step(eng.tensor_scalar(lg, lg, CAPACITY, 1.0, ALU.mult, ALU.min))
            step(eng.tensor_tensor(lg, lg, ex, ALU.mult))
            step(eng.tensor_reduce(r1, lg, AX.X, ALU.max))
            step(eng.tensor_scalar(lg, lg, r1, None, ALU.subtract))
            mark(ROUTE_SCALED)
            eng.wait_ge(route_act, 2)
            soft(NE)
            step(eng.tensor_scalar(ex, ex, r2, None, ALU.mult))
            step(eng.max(top, ex))
            step(eng.max_index(top_i, top, ex))
            mark(ROUTE_TOP)
            step(eng.tensor_scalar(lg[:, 0:2], top[:, 0:2], top[:, 0:1], None, ALU.subtract))
            mark(ROUTE_DIFF)
            eng.wait_ge(route_act, 3)
            soft(2)
            step(eng.tensor_scalar(lg[:, 2:4], ex[:, 0:2], r2, None, ALU.mult))
            mark(ROUTE_WEIGHTS)
            eng.wait_ge(b1_turned, 1)
            eng.tensor_copy(b1T, ptr[:, 0:2 * FT]).then_inc(b1_ready, 1)
            eng.wait_ge(route_pe, 2)
            step(eng.tensor_copy(wcol, pmisc[:, 0:2]))
            eng.wait_ge(expert_in, 16 * 8)
            for k in range(2):
                eng.tensor_scalar(w2e[:, k, :, :], w2e[:, k, :, :], wcol[:, k:k + 1], None, ALU.mult)
            step(eng.tensor_scalar(b2w[0:1, :], b2rows[0:1, 0, :], wcol[0:1, 0:1], None, ALU.mult))
            eng.scalar_tensor_tensor(out=b2w[0:1, :], in0=b2rows[0:1, 1, :], scalar=wcol[0:1, 1:2],
                                     in1=b2w[0:1, :], op0=ALU.mult, op1=ALU.add).then_inc(w2_ready, 1)

            def finish(t, half, i, bank, m):
                n = [0]

                def step(ins):
                    n[0] += 1
                    ins.then_inc(fin, 1)
                    eng.wait_ge(fin, FIN_N * t + n[0])
                z = zrow[i][0:m, :]
                z4 = z.rearrange("p (a b) -> p a b", a=4)
                eng.wait_ge(down_done, t + 1)
                eng.wait_ge(o_out[i], 16 * half + 16)
                eng.tensor_tensor(z4, bank[0:m, 0:D].rearrange("p (a b) -> p a b", a=4), xf_view(t, m),
                                  ALU.add).then_inc(y_read, 1)
                eng.wait_ge(y_read, t + 5)
                step(eng.bn_stats(stats[0:m, :], z))
                eng.sem_inc(passed_v, 1)
                step(eng.bn_aggr(mv[0:m, :], stats[0:m, :]))
                rsqrt_steps(eng, step, rs[0:m, :], rs_var[0:m, :], mv[0:m, 1:2], rs_tmp[0:m, :])
                step(eng.tensor_scalar(z, z, mv[0:m, 0:1], rs[0:m, :], ALU.subtract, ALU.mult))
                step(eng.tensor_tensor(z, z, gam[0:m, :], ALU.mult))
                step(eng.tensor_tensor(z, z, bet[0:m, :], ALU.add))
                eng.tensor_tensor(z4, z4, x1_view(t, m), ALU.add).then_inc(o_ready, 1)
                assert n[0] == FIN_N
            FIN_N = 5 + RSQRT_N
            ybank = [plin, ptr, pxf, pmisc]
            with eng.Fori(0, FGROUPS) as q:
                for i in range(4):
                    finish(4 * q + i, 2 * q + i // 2, i % 2, ybank[i], TN)
            finish(NT - 1, (NT - 1) // 2, 0, ybank[0], TLAST)


ROUTE_MEAN = 2
ROUTE_LOGITS = 5
ROUTE_SCALED = 14
ROUTE_TOP = 19
ROUTE_DIFF = 20
ROUTE_WEIGHTS = 23


_INS = ["x", "src", "dst", "edge_type_8", "L0_gnn_W1", "L0_gnn_self_w1", "L0_gnn_b1", "L0_gnn_W2", "L0_gnn_self_w2",
        "L0_gnn_b2", "L0_ffn_Wr", "L0_ffn_br", "L0_ffn_W1", "L0_ffn_b1", "L0_ffn_W2", "L0_ffn_b2", "L0_ffn_gamma",
        "L0_ffn_beta"]


def kernel(**inputs):
    import concourse.bacc as bacc
    from concourse.bass_utils import run_bass_kernel_spmd

    nc = bacc.Bacc("TRN2", target_bir_lowering=False, num_devices=1)
    arrays, ap = {}, {}
    for name in _INS:
        a = np.ascontiguousarray(inputs[name])
        arrays["in_" + name] = a
        ap[name] = nc.dram_tensor("in_" + name, a.shape, mybir.dt.from_np(a.dtype), kind="ExternalInput").ap()
    out = nc.dram_tensor("out_rows", (N, D), F32, kind="ExternalOutput").ap()
    program(nc, ap["x"], ap["src"], ap["dst"], ap["edge_type_8"], [ap["L0_gnn_W1"], ap["L0_gnn_W2"]],
            [ap["L0_gnn_self_w1"], ap["L0_gnn_self_w2"]], [ap["L0_gnn_b1"], ap["L0_gnn_b2"]], ap["L0_ffn_Wr"],
            ap["L0_ffn_br"], ap["L0_ffn_W1"], ap["L0_ffn_b1"], ap["L0_ffn_W2"], ap["L0_ffn_b2"], ap["L0_ffn_gamma"],
            ap["L0_ffn_beta"], out)
    result = run_bass_kernel_spmd(nc, [arrays], core_ids=[0])
    return result.results[0]["out_rows"]
```

```python
from contextlib import ExitStack

import numpy as np

import concourse.bass as bass
from concourse import mybir

F32 = mybir.dt.float32
I32 = mybir.dt.int32
F16 = mybir.dt.float16
U32 = mybir.dt.uint32
ALU = mybir.AluOpType
ACT = mybir.ActivationFunctionType
AX = mybir.AxisListType
DVE_ENGINE = mybir.EngineType.DVE

P = 128
N, D, R, E = 2500, 256, 8, 42500
F, NE = 512, 8
LN_EPS = 1e-5
CAPACITY = float(-(-N * 5 // (4 * NE)))

EC = 128
NCH = -(-E // EC)
CFULL = E // EC
CLAST = E - CFULL * EC
ROWS = -(-NCH // P)
CTAIL = NCH - (ROWS - 1) * P
NEWTON = [1.0, -0.5, 0.0625, -0.5 * 0.0625 ** 3]
RSQRT_N = 10
TN = 120
NT = -(-N // TN)
TLAST = N - (NT - 1) * TN
NPAD = NT * TN
WIN = 16
GC = 16
NG = NCH // GC
CREST = NCH - NG * GC
AHEAD = 3
LEAD = 5
GR = 8
SR = 4
NHALF = 2 * NG + 2
PASSES = -(-N // WIN)
BASE_MAX = NPAD - WIN
MM_CREDIT = 16
ADD_CREDIT = SR
INVALID = 65536.0
RSQRT_MAGIC = float(0x5F3759DF)
KT = D // P
FT = F // P
WSCALE = 64.0
FG = 4 * TN
FGROUPS = N // FG


def ready_chunks(t):
    return min(GC * (t + 1) + LEAD, NCH) if isinstance(t, int) else GC * (t + 1) + LEAD


def slot_uses(slot):
    return (NCH - slot + GR - 1) // GR


def program(nc, x, src, dst, etype, gW, gS, gB, Wr, br, W1, b1, W2, b2, gamma, beta, out):
    lnx = nc.dram_tensor("lnx", [N, D], F32, kind="Internal").ap()
    h1 = nc.dram_tensor("h1", [N, D], F32, kind="Internal").ap()
    table = [lnx, h1]

    ctx = ExitStack()
    with ctx:
        def sb(name, shape, dt=F32):
            return ctx.enter_context(nc.sbuf_tensor(name, shape, dt))

        def sem(name):
            return ctx.enter_context(nc.semaphore(name))

        agg = sb("agg", [P, KT, R, NPAD])
        bulk = sb("bulk", [P, NT, D])
        W = bulk[:, 0:KT * (R + 1), :]
        hout = bulk[:, 18, :]
        resid = bulk[:, 19, :]
        selfrow = bulk[:, 20, :]
        ring = sb("ring", [P, GR * D + SR * P])
        gath = [ring[:, i * D:(i + 1) * D] for i in range(GR)]
        onehot = [ring[:, GR * D + i * P:GR * D + (i + 1) * P] for i in range(SR)]
        edge_i = ring[:, 0:3 * ROWS * P].bitcast(I32).rearrange("p (a j e) -> p a j e", a=3, j=ROWS)
        stage = sb("stage", [P, KT * R, TN])
        edge_f = stage[:, :, :].rearrange("p k n -> p (k n)")[:, 0:3 * ROWS * P].rearrange(
            "p (a j e) -> p a j e", a=3, j=ROWS)
        selfT = sb("selfT", [P, KT, TN])
        xft32 = sb("xft32", [P, KT, TN])
        keyT = sb("keyT", [P, NCH])
        idx = sb("idx", [P, NCH], I32)
        idx_slot = sb("idx_slot", [P, 2 * GR], I32)
        base_row = sb("base_row", [1, ROWS * P], I32)
        ident = sb("ident", [P, P])
        pattern = sb("pattern", [P, P])
        pattern_i = sb("pattern_i", [P, P], I32)
        ones = sb("ones", [1, P])
        gbias = sb("gbias", [1, D])
        small = sb("small", [P, 128])
        colsum = sb("colsum", [P, KT, NT])

        pchunk = [ctx.enter_context(nc.psum_tensor(f"pchunk{i}", [P, 512], F32)) for i in range(SR)]
        plin = ctx.enter_context(nc.psum_tensor("plin", [P, 512], F32))
        ptr = ctx.enter_context(nc.psum_tensor("ptr", [P, 512], F32))
        pxf = ctx.enter_context(nc.psum_tensor("pxf", [P, 512], F32))
        pmisc = ctx.enter_context(nc.psum_tensor("pmisc", [P, 512], F32))

        edges_in = [sem(f"edges_in{a}") for a in range(3)]
        x_in = [sem(f"x_in{i}") for i in range(2)]
        consts = sem("consts")
        consts_v = sem("consts_v")
        edge_clear = sem("edge_clear")
        cleared = sem("cleared")
        lists_f = sem("lists_f")
        base_ready = sem("base_ready")
        keys = sem("keys")
        ln_stat = sem("ln_stat")
        pro = sem("pro")
        rows_ready = sem("rows_ready")
        check_ready = sem("check_ready")
        rows_turned = sem("rows_turned")
        turned_out = sem("turned_out")
        edges_ready = sem("edges_ready")
        ln_ready = sem("ln_ready")
        lnx_out = sem("lnx_out")
        w_in = sem("w_in")
        idx_ready = sem("idx_ready")
        gathered = [sem(f"gathered{i}") for i in range(GR)]
        onehot_ready = sem("onehot_ready")
        chunk_mm = sem("chunk_mm")
        chunk_add = sem("chunk_add")
        self_in = sem("self_in")
        self_turned = sem("self_turned")
        selfT_ready = sem("selfT_ready")
        staged = sem("staged")
        lin_done = sem("lin_done")
        h_ready = sem("h_ready")
        h_out = sem("h_out")
        resid_in = sem("resid_in")
        x1_ready = sem("x1_ready")
        tail = sem("tail")
        xf_ready = sem("xf_ready")
        xf_turned = sem("xf_turned")
        xfT_ready = sem("xfT_ready")
        gen_idx = sem("gen_idx")
        gen_in = sem("gen_in")
        gen_hot = [sem(f"gen_hot{L}") for L in range(2)]
        gen_mm = [sem(f"gen_mm{L}") for L in range(2)]
        gen_add = [sem(f"gen_add{L}") for L in range(2)]
        gen_win = [sem(f"gen_win{L}") for L in range(2)]
        gen_key = [sem(f"gen_key{L}") for L in range(2)]
        gen_clear = sem("gen_clear")
        route = sem("route")
        route_pe = sem("route_pe")
        route_act = sem("route_act")
        ffn_const_in = sem("ffn_const_in")
        expert_in = [sem(f"expert_in{e}") for e in range(2)]
        expert_rest = sem("expert_rest")
        w2_ready = sem("w2_ready")
        b1_turned = sem("b1_turned")
        b1_ready = sem("b1_ready")
        up_done = sem("up_done")
        gelu_done = sem("gelu_done")
        down_done = sem("down_done")
        w1_ready = [sem(f"w1_ready{e}") for e in range(2)]
        w2_high = sem("w2_high")
        wcol_ready = sem("wcol_ready")
        high_ready = sem("high_ready")
        low_ready = sem("low_ready")
        xf_high = sem("xf_high")
        y_read = sem("y_read")
        fin = sem("fin")
        o_ready = sem("o_ready")
        o_out = [sem(f"o_out{i}") for i in range(2)]

        key_now = small[:, 124:125]
        base_now = small[0:1, 125:126].bitcast(I32)
        passed = sem("passed")
        passed_v = sem("passed_v")
        passed_p = sem("passed_p")

        stats = small[:, 0:6]
        mv = small[:, 6:8]
        rs = small[:, 8:9]
        rs_var = small[:, 9:10]
        rs_tmp = small[:, 10:11]
        emin = small[:, 12:12 + ROWS]
        emax = small[:, 16:16 + ROWS]
        echk = small[:, 20:20 + ROWS]
        ebound = small[:, 24:24 + ROWS]
        ebound_i = small[:, 28:28 + ROWS].bitcast(I32)
        eupper = small[:, 84:84 + ROWS]
        eupper_i = small[:, 92:92 + ROWS].bitcast(I32)
        emaxi = small[:, 32:33]
        order_bad = small[0:1, 33:34].bitcast(I32)
        mean = small[:, 36:36 + KT]
        wcol = small[:, 40:42]
        b1T = small[:, 48:48 + 2 * FT]
        lg = small[0:1, 56:64]
        ex = small[0:1, 64:72]
        top = small[0:1, 72:80]
        top_i = small[0:1, 80:88].bitcast(U32)
        r1 = small[0:1, 88:89]
        r2 = small[0:1, 89:90]
        zero = small[:, 126:127].rearrange("p (a b) -> p a b", a=1)
        brow = small[0:1, 96:104]
        sumc = small[:, 104:104 + KT]
        WrT = small[:, 108:108 + KT * NE].rearrange("p (k e) -> p k e", k=KT)

        def x1_view(t, m):
            return agg[0:m, 0, 0:4, bass.ds(TN * t, 64)]

        def xf_view(t, m):
            return agg[0:m, 0, 4:8, bass.ds(TN * t, 64)]

        xfT = [agg[:, 1, h, :].bitcast(F16).rearrange("p (t s n) -> p t s n", s=2, n=TN) for h in range(KT)]
        late = agg[:, 1, KT:R, :].rearrange("p r n -> p (r n)")
        at = 0

        def carve(cols):
            nonlocal at
            at += cols
            assert at <= (R - KT) * NPAD
            return late[:, at - cols:at]
        w1s = carve(2 * KT * F).bitcast(F16).rearrange("p (e s k f) -> p e s k f", e=2, s=2, k=KT)
        w2s = carve(2 * FT * D).bitcast(F16).rearrange("p (e s k d) -> p e s k d", e=2, s=2, k=FT)
        hid = carve(2 * 2 * FT * FG).bitcast(F16).rearrange("p (b k s n) -> p b k s n", b=2, k=2 * FT, s=2)
        flat = bulk[:, :, :].rearrange("p t d -> p (t d)")
        w1e = flat[:, 0:2 * KT * F].rearrange("p (e k f) -> p e k f", e=2, k=KT)
        w2e = flat[:, 2 * KT * F:2 * KT * F + 2 * FT * D].rearrange("p (e k d) -> p e k d", e=2, k=FT)
        g32 = [ring[:, i * FG:(i + 1) * FG] for i in range(2)]
        gam = carve(D)
        bet = carve(D)
        b1rows = carve(P)
        b2rows = carve(2 * D).rearrange("p (e d) -> p e d", e=2)
        b2w = carve(D)
        zrow = [carve(D), carve(D)]

        ln_stats = keyT[:, 0:6 * NT].rearrange("p (t s) -> p t s", s=6)
        ln_mv = keyT[:, 6 * NT:8 * NT].rearrange("p (t s) -> p t s", s=2)
        ln_rs = keyT[:, 8 * NT:9 * NT]
        ln_var = keyT[:, 9 * NT:10 * NT]
        ln_tmp = keyT[:, 10 * NT:11 * NT]
        ln_shift = keyT[:, 11 * NT:12 * NT]

        block = ctx.enter_context(nc.Block())

        def rsqrt_steps(eng, step, y, v, var, tmp):
            yi, vi = y.bitcast(I32), v.bitcast(I32)
            step(eng.tensor_scalar(v, var, LN_EPS, None, ALU.add))
            step(eng.tensor_scalar(yi, vi, 1, None, ALU.arith_shift_right))
            step(eng.tensor_scalar(yi, yi, -1.0, RSQRT_MAGIC, ALU.mult, ALU.add))
            for _ in range(3):
                step(eng.tensor_tensor(tmp, y, y, ALU.mult))
                step(eng.tensor_tensor(tmp, tmp, v, ALU.mult))
                step(eng.tensor_scalar(tmp, tmp, -0.5, 1.5, ALU.mult, ALU.add))
                step(eng.tensor_tensor(y, y, tmp, ALU.mult))

        def rsqrt_step(eng, k, m):
            y, v, t = rs[0:m, :], rs_var[0:m, :], rs_tmp[0:m, :]
            if k == 0:
                return eng.tensor_scalar(v, mv[0:m, 1:2], LN_EPS, None, ALU.add)
            if k == 1:
                return eng.tensor_scalar(y.bitcast(I32), v.bitcast(I32), 1, None, ALU.arith_shift_right)
            if k == 2:
                return eng.tensor_scalar(y.bitcast(I32), y.bitcast(I32), -1.0, RSQRT_MAGIC, ALU.mult, ALU.add)
            if k == RSQRT_N - 1:
                return eng.tensor_scalar(y, y, NEWTON[3], None, ALU.mult)
            a = NEWTON[(k - 3) // 2]
            if k % 2:
                return eng.scalar_tensor_tensor(out=t, in0=y, scalar=y, in1=v, op0=ALU.mult, op1=ALU.mult)
            return eng.scalar_tensor_tensor(out=y, in0=t, scalar=3.0 / (a * a), in1=y, op0=ALU.subtract, op1=ALU.mult)

        XB = [(0, 10), (10, NT)]

        @block.sync
        def _(eng):
            lists = (dst, etype, src)
            for a, lst in enumerate(lists):
                full = (ROWS - 1) * P * EC
                eng.dma_start(edge_i[:, a, 0:ROWS - 1, :],
                              lst[0:full].rearrange("(j p e) -> p j e", p=P, e=EC)).then_inc(edges_in[a], 16)
            eng.wait_ge(edge_clear, 1)
            for a, lst in enumerate(lists):
                full = (ROWS - 1) * P * EC
                eng.dma_start(edge_i[0:CTAIL - 1, a, ROWS - 1, :],
                              lst[full:CFULL * EC].rearrange("(p e) -> p e", e=EC)).then_inc(edges_in[a], 16)
                if a == 0:
                    eng.dma_start(edge_i[CTAIL - 1:CTAIL, a, ROWS - 1, :],
                                  lst[E - EC:E].rearrange("(p e) -> p e", p=1)).then_inc(edges_in[a], 16)
                else:
                    eng.dma_start(edge_i[CTAIL - 1:CTAIL, a, ROWS - 1, EC - CLAST:EC],
                                  lst[E - CLAST:E].rearrange("(p e) -> p e", p=1)).then_inc(edges_in[a], 16)
            eng.dma_start(WrT, Wr.rearrange("(k p) e -> p k e", p=P)).then_inc(ffn_const_in, 16)
            eng.dma_start(brow, br.rearrange("(a e) -> a e", a=1)).then_inc(ffn_const_in, 16)
            for b, (t0, t1) in enumerate(XB):
                eng.wait_ge(ln_ready, b + 1)
                tf = min(t1, NT - 1)
                eng.dma_start(lnx[t0 * TN:tf * TN, :].rearrange("(t p) d -> p t d", p=TN),
                              bulk[0:TN, t0:tf, :]).then_inc(lnx_out, 16)
            eng.dma_start(lnx[(NT - 1) * TN:N, :], bulk[0:TLAST, NT - 1, :]).then_inc(lnx_out, 16)

            def load_weights(L):
                eng.dma_start(W[:, 0:KT * R, :], gW[L].rearrange("r (h p) o -> p (r h) o", p=P)).then_inc(w_in, 16)
                eng.dma_start(W[:, KT * R:, :], gS[L].rearrange("(h p) o -> p h o", p=P)).then_inc(w_in, 16)
                eng.dma_start(gbias[:, :], gB[L].rearrange("(a d) -> a d", a=1)).then_inc(w_in, 16)

            def load_rows(L, t, m):
                T = L * NT + t
                eng.wait_ge(self_turned, T + 1)
                eng.dma_start(selfrow[0:m, :], table[L][bass.ds(TN * t, m), :]).then_inc(self_in, 16)
                if L == 1:
                    eng.wait_ge(x1_ready, t + 1)
                    eng.dma_start(resid[0:m, :], x[bass.ds(TN * t, m), :]).then_inc(resid_in, 16)

            def store_h(t, m):
                eng.wait_ge(h_ready, t + 2)
                eng.dma_start(h1[bass.ds(TN * t, m), :], hout[0:m, :]).then_inc(h_out, 16)

            for L in range(2):
                if L == 0:
                    eng.wait_ge(lnx_out, 48)
                else:
                    eng.wait_ge(h_out, 16 * NT + 16)
                    eng.wait_ge(lin_done, NT + 1)
                load_weights(L)
                with eng.Fori(0, NT - 1) as t:
                    load_rows(L, t, TN)
                    if L == 0:
                        store_h(t, TN)
                load_rows(L, NT - 1, TLAST)
                if L == 0:
                    store_h(NT - 1, TLAST)
            eng.wait_ge(lin_done, 2 * NT + 1)
            eng.dma_start(gam, gamma.rearrange("(a d) -> a d", a=1).to_broadcast([P, D])).then_inc(ffn_const_in, 16)
            eng.dma_start(bet, beta.rearrange("(a d) -> a d", a=1).to_broadcast([P, D])).then_inc(ffn_const_in, 16)
            eng.wait_ge(route, ROUTE_TOP)
            ex_i = [eng.value_load(top_i[0:1, k:k + 1], min_val=0, max_val=NE - 1) for k in range(2)]
            for k, e in enumerate(ex_i):
                eng.dma_start(w1e[:, k, :, :],
                              W1[bass.ds(e, 1), :, :].rearrange("a (k p) f -> p (a k) f", p=P)).then_inc(expert_in[k], 16)
            for k, e in enumerate(ex_i):
                eng.dma_start(b1rows[FT * k:FT * (k + 1), :],
                              b1[bass.ds(e, 1), :].rearrange("a (k p) -> (a k) p", p=P)).then_inc(expert_rest, 16)
                eng.dma_start(b2rows[0:1, k, :], b2[bass.ds(e, 1), :]).then_inc(expert_rest, 16)
                eng.dma_start(w2e[:, k, :, :],
                              W2[bass.ds(e, 1), :, :].rearrange("a (k p) d -> p (a k) d", p=P)).then_inc(expert_rest, 16)
            with eng.Fori(0, (NT - 1) // 2) as u:
                for i in range(2):
                    eng.wait_ge(o_ready, 2 * u + i + 1)
                    eng.dma_start(out[bass.ds(TN * (2 * u + i), TN), :], zrow[i][0:TN, :]).then_inc(o_out[i], 16)
            eng.wait_ge(o_ready, NT)
            eng.dma_start(out[(NT - 1) * TN:N, :], zrow[0][0:TLAST, :]).then_inc(o_out[0], 16)
            eng.wait_ge(o_out[0], 16 * ((NT - 1) // 2 + 1) + 16)
            eng.wait_ge(o_out[1], 16 * ((NT - 1) // 2) + 16)

        @block.gpsimd
        def _(eng):
            eng.memset(ident[:, :], 0.0).then_inc(consts, 1)
            eng.iota(pattern_i[:, :], pattern=[[1, R], [R, WIN]], base=0, channel_multiplier=0).then_inc(consts, 1)
            eng.iota(ebound_i[:, :], pattern=[[P, ROWS]], base=-LEAD, channel_multiplier=1).then_inc(consts, 1)
            eng.iota(eupper_i[:, :], pattern=[[P, ROWS]], base=0, channel_multiplier=1).then_inc(consts, 1)
            eng.wait_ge(consts, 1)
            eng.affine_select(out=ident[:, :], in_=ident[:, :], compare_op=ALU.not_equal, fill=1.0,
                              base=0, pattern=[[-1, P]], channel_multiplier=1).then_inc(consts, 1)
            for a in range(3):
                eng.wait_ge(edges_in[a], 48)
                eng.tensor_copy(edge_f[:, a, :, :], edge_i[:, a, :, :]).then_inc(lists_f, 1)
            eng.wait_ge(base_ready, 1)
            for j in range(ROWS):
                eng.tensor_scalar(edge_f[:, 0, j, :], edge_f[:, 0, j, :], emin[:, j:j + 1], float(R),
                                  ALU.subtract, ALU.mult).then_inc(keys, 1)
            eng.wait_ge(keys, ROWS)
            eng.tensor_tensor(edge_f[:, 1, :, :], edge_f[:, 1, :, :], edge_f[:, 0, :, :],
                              ALU.add).then_inc(rows_ready, 1)
            eng.wait_ge(edges_ready, 1)
            bad = eng.value_load(order_bad, min_val=0, max_val=1)
            with eng.If(bad == 0):
                for L in range(2):
                    def gather(g, j):
                        s = j % GR
                        eng.wait_ge(idx_ready, L * NHALF + 2 * g + j // GR + 1)
                        eng.wait_ge(chunk_mm, MM_CREDIT + L * NCH + GC * g + j - GR + 1)
                        eng.sem_inc(passed, 1)
                        eng.indirect_dma_start(out=gath[s], out_offset=None, in_=table[L][:, :],
                                               in_offset=bass.IndirectOffsetOnAxis(
                                                   ap=idx_slot[:, j:j + 1], axis=0)).then_inc(gathered[s], 16)
                    if L == 0:
                        eng.wait_ge(lnx_out, 48)
                    else:
                        eng.wait_ge(h_out, 16 * NT + 16)
                    with eng.Fori(0, NG) as g:
                        for j in range(GC):
                            gather(g, j)
                    for j in range(CREST):
                        gather(NG, j)
            with eng.Else():
                for L in range(2):
                    if L == 0:
                        eng.wait_ge(lnx_out, 48)
                    else:
                        eng.wait_ge(h_out, 16 * NT + 16)
                    with eng.Fori(0, NCH) as c:
                        eng.wait_ge(gen_mm[L], PASSES * c + 1)
                        eng.tensor_copy(idx_slot[:, 0:1], idx[:, bass.ds(c, 1)]).then_inc(gen_idx, 1)
                        eng.wait_ge(gen_idx, L * NCH + c + 1)
                        eng.sem_inc(passed, 1)
                        eng.indirect_dma_start(out=gath[0], out_offset=None, in_=table[L][:, :],
                                               in_offset=bass.IndirectOffsetOnAxis(
                                                   ap=idx_slot[:, 0:1], axis=0)).then_inc(gen_in, 16)

            def lows(q, buf, m):
                for k in range(2 * FT):
                    eng.wait_ge(high_ready, 2 * FT * q + k + 1)
                    eng.tensor_tensor(hid[:, buf, k, 1, 0:m], g32[k % 2][:, 0:m], hid[:, buf, k, 0, 0:m],
                                      ALU.subtract).then_inc(low_ready, 1)
            lows(0, 0, FG)
            with eng.Fori(0, (FGROUPS - 1) // 2) as u:
                lows(2 * u + 1, 1, FG)
                lows(2 * u + 2, 0, FG)
            lows(FGROUPS, 1, TLAST)

        @block.scalar
        def _(eng):
            for b, (t0, t1) in enumerate(XB):
                tf = min(t1, NT - 1)
                eng.dma_start(bulk[0:TN, t0:tf, :],
                              x[t0 * TN:tf * TN, :].rearrange("(t p) d -> p t d", p=TN)).then_inc(x_in[b], 16)
            eng.dma_start(bulk[0:TLAST, NT - 1, :], x[(NT - 1) * TN:N, :]).then_inc(x_in[1], 16)
            eng.wait_ge(consts_v, 1)
            eng.activation(agg[:, :, :, 0:AHEAD * TN].rearrange("p h r n -> p (h r) n"),
                           zero.to_broadcast([P, KT * R, AHEAD * TN]), ACT.Copy).then_inc(cleared, 1)
            for b, (t0, t1) in enumerate(XB):
                eng.wait_ge(ln_stat, b + 1)
                for t in range(t0, t1):
                    m = TN if t < NT - 1 else TLAST
                    ins = eng.activation(bulk[0:m, t, :], bulk[0:m, t, :], ACT.Identity, bias=ln_shift[0:m, t:t + 1],
                                         scale=ln_rs[0:m, t:t + 1])
                ins.then_inc(ln_ready, 1)

            def turn_self(L, t, m):
                T = L * NT + t
                eng.wait_ge(self_turned, T + 2)
                eng.wait_ge(lin_done, T + 1)
                eng.activation(selfT[:, :, 0:m], ptr[:, 0:KT * m].rearrange("p (k n) -> p k n", k=KT),
                               ACT.Copy).then_inc(selfT_ready, 1)

            def stage_tile(L, t, m):
                T = L * NT + t
                eng.wait_ge(lin_done, T + 1)
                eng.activation(stage[:, :, 0:m],
                               agg[:, :, :, bass.ds(TN * t, m)].rearrange("p h r n -> p (h r) n"),
                               ACT.Copy).then_inc(staged, 1)

            def relu_rows(t, m):
                eng.wait_ge(lin_done, t + 2)
                eng.wait_ge(h_out, 16 * t + 16)
                eng.activation(hout[0:m, :], plin[0:m, 0:D], ACT.Relu).then_inc(h_ready, 1)

            def keep_xfT(t, m):
                eng.wait_ge(xf_turned, t + 2)
                eng.wait_ge(xfT_ready, t + 1)
                for h in range(KT):
                    eng.activation(xft32[:, h, 0:m], pxf[:, h * TN:h * TN + m], ACT.Identity,
                                   accum_out=colsum[:, h, bass.ds(t, 1)])
                for h in range(KT):
                    ins = eng.activation(xfT[h][:, bass.ds(t, 1), 0, 0:m].rearrange("p a n -> p (a n)"),
                                         pxf[:, h * TN:h * TN + m], ACT.Copy)
                ins.then_inc(xf_high, 1)

            def clear_columns(t, tiles):
                eng.activation(agg[:, :, :, bass.ds(TN * t, TN * tiles)].rearrange("p h r n -> p (h r) n"),
                               zero.to_broadcast([P, KT * R, TN * tiles]), ACT.Copy).then_inc(cleared, 1)

            def copy_indices(L, half, c0, cols):
                eng.wait_ge(chunk_mm, MM_CREDIT + L * NCH + c0 - GR)
                eng.activation(idx_slot[:, half * GR:half * GR + cols], idx[:, bass.ds(c0, cols)],
                               ACT.Copy).then_inc(idx_ready, 1)

            eng.wait_ge(edges_ready, 1)
            bad = eng.value_load(order_bad, min_val=0, max_val=1)
            with eng.If(bad == 0):
                for L in range(2):
                    def group(g, lin=None, end=None, clear=False, copies=(GR, GR)):
                        if lin is not None:
                            turn_self(L, lin, TN)
                            eng.wait_ge(chunk_add, ADD_CREDIT + L * NCH + ready_chunks(lin))
                            stage_tile(L, lin, TN)
                        if copies:
                            copy_indices(L, 0, GC * g + GC, copies[0])
                        if clear:
                            clear_columns(g + AHEAD, 1)
                        if L == 0 and lin is not None:
                            relu_rows(lin, TN)
                        if L == 1 and end is not None:
                            keep_xfT(end, TN)
                        if copies:
                            copy_indices(L, 1, GC * g + GC + GR, copies[1])

                    if L == 1:
                        eng.wait_ge(chunk_mm, MM_CREDIT + NCH)
                    copy_indices(L, 0, 0, GR)
                    copy_indices(L, 1, GR, GR)
                    group(0, clear=True)
                    group(1, lin=0, clear=True)
                    with eng.Fori(2, NT - AHEAD) as g:
                        group(g, lin=g - 1, end=g - 2, clear=True)
                    for g in range(NT - AHEAD, NG - 1):
                        group(g, lin=g - 1, end=g - 2)
                    group(NG - 1, lin=NG - 2, end=NG - 3, copies=(GR, CREST - GR))
                    if L == 0:
                        clear_columns(0, AHEAD)
                    group(NG, lin=NT - 2, end=NT - 3, copies=None)
                    if L == 1:
                        turn_self(L, NT - 1, TLAST)
                        eng.wait_ge(chunk_add, ADD_CREDIT + L * NCH + NCH)
                        stage_tile(L, NT - 1, TLAST)
                        keep_xfT(NT - 2, TN)
                        keep_xfT(NT - 1, TLAST)
                    else:
                        turn_self(L, NT - 1, TLAST)
                        eng.wait_ge(chunk_add, ADD_CREDIT + L * NCH + NCH)
                        stage_tile(L, NT - 1, TLAST)
                        relu_rows(NT - 1, TLAST)
            with eng.Else():
                for L in range(2):
                    eng.wait_ge(gen_add[L], PASSES * NCH + 1)

                    def tile(t, m):
                        turn_self(L, t, m)
                        stage_tile(L, t, m)
                        if L == 0:
                            relu_rows(t, m)
                        else:
                            keep_xfT(t, m)
                    with eng.Fori(0, NT - 1) as t:
                        tile(t, TN)
                    tile(NT - 1, TLAST)
            eng.wait_ge(route, ROUTE_LOGITS)
            eng.activation(ex, lg, ACT.Exp).then_inc(route_act, 1)
            eng.wait_ge(route, ROUTE_SCALED)
            eng.activation(ex, lg, ACT.Exp).then_inc(route_act, 1)
            eng.wait_ge(route, ROUTE_DIFF)
            eng.activation(ex[:, 0:2], lg[:, 0:2], ACT.Exp).then_inc(route_act, 1)
            for e in range(2):
                eng.wait_ge(expert_in[e], 16)
                eng.activation(w1s[:, e, 0, :, :], w1e[:, e, :, :], ACT.Copy, scale=WSCALE).then_inc(w1_ready[e], 1)
            eng.wait_ge(wcol_ready, 1)
            eng.wait_ge(expert_rest, 16 * 6)
            for e in range(2):
                eng.activation(w2s[:, e, 0, :, :], w2e[:, e, :, :], ACT.Copy, scale=wcol[:, e:e + 1]).then_inc(w2_high, 1)
            eng.wait_ge(b1_ready, 1)

            def gelu(q, buf, m):
                for k in range(2 * FT):
                    eng.wait_ge(up_done, 2 * FT * q + k + 1)
                    eng.wait_ge(low_ready, 2 * FT * q + k + 1)
                    eng.activation(g32[k % 2][:, 0:m], pchunk[k % SR][:, 0:m], ACT.Gelu, bias=b1T[:, k:k + 1],
                                   scale=1.0 / WSCALE).then_inc(gelu_done, 1)
                    eng.wait_ge(gelu_done, SR + 2 * FT * q + k + 1)
                    eng.activation(hid[:, buf, k, 0, 0:m], g32[k % 2][:, 0:m], ACT.Copy).then_inc(high_ready, 1)
            gelu(0, 0, FG)
            with eng.Fori(0, (FGROUPS - 1) // 2) as u:
                gelu(2 * u + 1, 1, FG)
                gelu(2 * u + 2, 0, FG)
            gelu(FGROUPS, 1, TLAST)

        @block.tensor
        def _(eng):
            eng.wait_ge(consts, 5)
            eng.wait_ge(rows_ready, 1)
            blocks = [(a, j) for a in range(2) for j in range(ROWS)]
            for n, (a, j) in enumerate(blocks):
                m = P if j < ROWS - 1 else CTAIL
                if n >= SR:
                    eng.wait_ge(turned_out, n - SR + 1)
                eng.transpose(pchunk[n % SR][:, 0:m], edge_f[0:m, a + 1, j, :], ident[0:m, 0:m]).then_inc(rows_turned, 1)
            for j in range(ROWS):
                ins = eng.transpose(plin[0:1, j * P:(j + 1) * P], emin[:, j:j + 1], ident[:, :])
            ins.then_inc(rows_turned, 1)
            eng.wait_ge(check_ready, 1)
            eng.transpose(ptr[0:1, 0:P], emaxi, ident[:, :]).then_inc(rows_turned, 1)
            eng.wait_ge(edges_ready, 1)
            bad = eng.value_load(order_bad, min_val=0, max_val=1)

            def turn_self(L, t, m):
                T = L * NT + t
                eng.wait_ge(self_in, 16 * T + 16)
                eng.wait_ge(selfT_ready, T + 1)
                for h in range(KT):
                    ins = eng.transpose(ptr[:, h * m:(h + 1) * m], selfrow[0:m, h * P:(h + 1) * P], ident[0:m, 0:m])
                ins.then_inc(self_turned, 1)

            def products(L, t, m, k0, k1):
                T = L * NT + t
                for k in range(k0, k1):
                    if k == 0:
                        if L == 0:
                            eng.wait_ge(h_ready, t + 1)
                        else:
                            eng.wait_ge(h_ready, NT + 1)
                            eng.wait_ge(x1_ready, t + 1)
                        eng.matmul(plin[0:m, 0:D], ones[0:1, 0:m], gbias[0:1, :], start=True, stop=False)
                    elif k <= KT:
                        if k == 1:
                            eng.wait_ge(selfT_ready, T + 2)
                        eng.matmul(plin[0:m, 0:D], selfT[:, k - 1, 0:m], W[:, KT * R + k - 1, :], start=False, stop=False)
                    else:
                        if k == KT + 1:
                            eng.wait_ge(staged, T + 1)
                        h, r = (k - KT - 1) // R, (k - KT - 1) % R
                        ins = eng.matmul(plin[0:m, 0:D], stage[:, h * R + r, 0:m], W[:, KT * r + h, :],
                                         start=False, stop=(k == KT * (R + 1)))
                        if k == KT * (R + 1):
                            ins.then_inc(lin_done, 1)
            STEPS = KT * (R + 1) + 1

            def turn_xf(t, m):
                eng.wait_ge(xf_ready, t + 1)
                eng.wait_ge(xfT_ready, t + 1)
                for h in range(KT):
                    ins = eng.transpose(pxf[:, h * TN:h * TN + m], hout[0:m, h * P:(h + 1) * P], ident[0:m, 0:m])
                ins.then_inc(xf_turned, 1)

            with eng.If(bad == 0):
                for L in range(2):
                    def chunk(g, j):
                        s = j % GR
                        first = j // GR + 1 + L * slot_uses(s)
                        eng.wait_ge(gathered[s], 16 * (2 * g + first))
                        eng.wait_ge(onehot_ready, L * NCH + GC * g + j + 1)
                        eng.wait_ge(chunk_add, L * NCH + GC * g + j + 1)
                        for h in range(KT):
                            ins = eng.matmul(pchunk[j % SR][:, h * P:(h + 1) * P], gath[s][:, h * P:(h + 1) * P],
                                             onehot[j % SR], start=True, stop=True)
                        ins.then_inc(chunk_mm, 1)

                    def group(g, chunks, lin=None, end=None):
                        step = 0
                        for j in range(chunks):
                            chunk(g, j)
                            if j == 10 and L == 1 and end is not None:
                                turn_xf(end, TN)
                            if lin is None:
                                continue
                            if j == 3:
                                turn_self(L, lin, TN)
                            if j >= 7:
                                to = min(-(-STEPS * (j - 6) // min(chunks - 7, 7)), STEPS)
                                products(L, lin, TN, step, to)
                                step = to

                    eng.wait_ge(chunk_add, ADD_CREDIT + L * NCH)
                    group(0, GC)
                    eng.wait_ge(w_in, 48 * (L + 1))
                    group(1, GC, lin=0)
                    with eng.Fori(2, NG) as g:
                        group(g, GC, lin=g - 1, end=g - 2)
                    group(NG, CREST, lin=NT - 2, end=NT - 3)
                    turn_self(L, NT - 1, TLAST)
                    products(L, NT - 1, TLAST, 0, STEPS)
                    if L == 1:
                        turn_xf(NT - 2, TN)
                        turn_xf(NT - 1, TLAST)
            with eng.Else():
                for L in range(2):
                    with eng.Fori(0, NCH) as c:
                        eng.wait_ge(gen_in, 16 * (L * NCH + c) + 16)
                        eng.sem_inc(passed_p, 1)
                        with eng.Fori(0, PASSES) as k:
                            eng.wait_ge(gen_hot[L], PASSES * c + k + 1)
                            eng.wait_ge(gen_add[L], PASSES * c + k + 1)
                            for h in range(KT):
                                ins = eng.matmul(pchunk[0][:, h * P:(h + 1) * P], gath[0][:, h * P:(h + 1) * P],
                                                 onehot[0], start=True, stop=True)
                            ins.then_inc(gen_mm[L], 1)
                    eng.wait_ge(w_in, 48 * (L + 1))

                    def tile(t, m):
                        turn_self(L, t, m)
                        products(L, t, m, 0, STEPS)
                        if L == 1:
                            turn_xf(t, m)
                    with eng.Fori(0, NT - 1) as t:
                        tile(t, TN)
                    tile(NT - 1, TLAST)
            eng.wait_ge(ffn_const_in, 64)
            eng.wait_ge(route, ROUTE_MEAN)
            for k in range(KT):
                ins = eng.matmul(pmisc[0:1, 0:NE], mean[:, k:k + 1], WrT[:, k, :], start=(k == 0), stop=(k == KT - 1))
            ins.then_inc(route_pe, 1)
            eng.wait_ge(expert_rest, 16 * 6)
            eng.transpose(ptr[:, 0:2 * FT], b1rows[0:2 * FT, :], ident[0:2 * FT, 0:2 * FT]).then_inc(b1_turned, 1)
            eng.wait_ge(route, ROUTE_WEIGHTS)
            eng.matmul(pmisc[:, 0:2], ones[0:1, :], lg[:, 2:4], start=True, stop=True).then_inc(route_pe, 1)

            ybank = [plin, ptr, pxf, pmisc]

            def up(q, m):
                for k in range(2 * FT):
                    e, f = k // FT, k % FT
                    eng.wait_ge(gelu_done, 2 * FT * q + k + 1)
                    n = 0
                    for sw, sx in ((0, 0), (0, 1), (1, 0)):
                        for i in range(KT):
                            tiles, cols = (4, TN) if m == FG else (1, m)
                            ins = eng.matmul(pchunk[k % SR][:, 0:m].rearrange("p (t n) -> p t n", t=tiles),
                                             w1s[:, e, sw, i, f * P:(f + 1) * P],
                                             xfT[i][:, bass.ds(4 * q, tiles), sx, 0:cols], start=(n == 0), stop=(n == 5))
                            n += 1
                    ins.then_inc(up_done, 1)

            def down(q, buf, tiles):
                for i, mt in enumerate(tiles):
                    eng.wait_ge(y_read, 4 * q + i + 1)
                    eng.matmul(ybank[i][0:mt, 0:D], ones[0:1, 0:mt], b2w[0:1, :], start=True, stop=False)
                    for k in range(2 * FT):
                        if i == 0:
                            eng.wait_ge(low_ready, 2 + 2 * FT * q + k + 1)
                        for sh, sw in ((0, 0), (0, 1), (1, 0)):
                            ins = eng.matmul(ybank[i][0:mt, 0:D], hid[:, buf, k, sh, i * TN:i * TN + mt],
                                             w2s[:, k // FT, sw, k % FT, :], start=False,
                                             stop=(k == 2 * FT - 1 and sh == 1))
                    ins.then_inc(down_done, 1)
            eng.wait_ge(xfT_ready, NT + 1)
            for e in range(2):
                eng.wait_ge(w1_ready[e], 2)
            up(0, FG)
            eng.wait_ge(w2_ready, 1)
            with eng.Fori(0, (FGROUPS - 1) // 2) as u:
                up(2 * u + 1, FG)
                down(2 * u, 0, [TN] * 4)
                up(2 * u + 2, FG)
                down(2 * u + 1, 1, [TN] * 4)
            up(FGROUPS, TLAST)
            down(FGROUPS - 1, 0, [TN] * 4)
            down(FGROUPS, 1, [TLAST])

        @block.vector
        def _(eng):
            eng.sem_inc(chunk_mm, MM_CREDIT)
            eng.sem_inc(chunk_add, ADD_CREDIT)
            for s in (self_turned, selfT_ready, lin_done, h_ready, x1_ready, xfT_ready, xf_turned, *gen_mm, *gen_add, *gen_win, *gen_key):
                eng.sem_inc(s, 1)
            for s in (h_out, o_out[0], o_out[1]):
                eng.sem_inc(s, 16)
            eng.sem_inc(gelu_done, SR)
            eng.sem_inc(y_read, 4)
            eng.sem_inc(low_ready, 2)

            count = [0]

            def step(ins):
                count[0] += 1
                ins.then_inc(pro, 1)
                eng.wait_ge(pro, count[0])

            def bases():
                eng.wait_ge(lists_f, 1)
                eng.tensor_reduce(emin, edge_f[:, 0, :, :], AX.X, ALU.min).then_inc(pro, 1)
                count[0] += 1
                step(eng.tensor_reduce(emax, edge_f[:, 0, :, :], AX.X, ALU.max))
                eng.sem_inc(base_ready, 1)

            def order_check():
                step(eng.tensor_scalar(ebound_i, ebound_i, GC.bit_length() - 1, None, ALU.arith_shift_right))
                step(eng.tensor_scalar(eupper_i, eupper_i, GC.bit_length() - 1, None, ALU.arith_shift_right))
                step(eng.tensor_scalar(ebound, ebound_i, float(TN), None, ALU.mult))
                step(eng.tensor_scalar(eupper, eupper_i, float(TN), float(AHEAD * TN - WIN), ALU.mult, ALU.add))
                step(eng.tensor_tensor(ebound, ebound, emin, ALU.subtract))
                step(eng.tensor_tensor(eupper, emin, eupper, ALU.subtract))
                step(eng.tensor_tensor(emax, emax, emin, ALU.subtract))
                step(eng.tensor_scalar(emax, emax, float(WIN - 1), None, ALU.subtract))
                step(eng.tensor_tensor(emax, emax, ebound, ALU.max))
                for j in range(ROWS):
                    m = P if j < ROWS - 1 else CTAIL
                    ins = eng.tensor_tensor(echk[0:m, j:j + 1], emax[0:m, j:j + 1], eupper[0:m, j:j + 1], ALU.max)
                step(ins)
                eng.tensor_reduce(emaxi, echk, AX.X, ALU.max).then_inc(check_ready, 1)

            eng.memset(edge_i[:, 0, ROWS - 1, :], 0)
            eng.memset(edge_i[:, 2, ROWS - 1, :], 0)
            eng.memset(edge_i[:, 1, ROWS - 1, :], int(INVALID)).then_inc(edge_clear, 1)
            eng.memset(small[:, 126:127], 0.0).then_inc(consts_v, 1)
            eng.memset(ones[:, :], 1.0).then_inc(consts_v, 1)
            eng.memset(echk[:, :], -1.0).then_inc(consts_v, 1)
            eng.memset(ln_mv[:, NT - 1, :], 1.0).then_inc(consts_v, 1)

            eng.wait_ge(consts_v, 4)
            for b, (t0, t1) in enumerate(XB):
                eng.wait_ge(x_in[b], 16 * (b + 1))
                for t in range(t0, t1):
                    m = TN if t < NT - 1 else TLAST
                    ins = eng.bn_stats(ln_stats[0:m, t, :], bulk[0:m, t, :])
                step(ins)
                for t in range(t0, t1):
                    m = TN if t < NT - 1 else TLAST
                    ins = eng.bn_aggr(ln_mv[0:m, t, :], ln_stats[0:m, t, :])
                step(ins)
                rsqrt_steps(eng, step, ln_rs[0:TN, t0:t1], ln_var[0:TN, t0:t1], ln_mv[0:TN, t0:t1, 1],
                            ln_tmp[0:TN, t0:t1])
                eng.scalar_tensor_tensor(out=ln_shift[0:TN, t0:t1], in0=ln_mv[0:TN, t0:t1, 0], scalar=-1.0,
                                         in1=ln_rs[0:TN, t0:t1], op0=ALU.mult, op1=ALU.mult).then_inc(ln_stat, 1)
                if b == 0:
                    bases()
            eng.wait_ge(consts, 5)
            step(eng.tensor_copy(pattern[:, :], pattern_i[:, :]))
            order_check()
            eng.wait_ge(ln_ready, len(XB))
            blocks = [(a, j) for a in range(2) for j in range(ROWS)]
            for n, (a, j) in enumerate(blocks):
                m = P if j < ROWS - 1 else CTAIL
                eng.wait_ge(rows_turned, n + 1)
                to = keyT if a == 0 else idx
                ins = eng.tensor_copy(to[:, j * P:j * P + m], pchunk[n % SR][:, 0:m]).then_inc(turned_out, 1)
            eng.wait_ge(rows_turned, len(blocks) + 2)
            step(eng.tensor_copy(base_row[:, :], plin[0:1, 0:ROWS * P]))
            step(eng.tensor_reduce(r1, ptr[0:1, 0:P], AX.X, ALU.max))
            step(eng.tensor_scalar(order_bad, r1, 0.5, None, ALU.is_gt))
            eng.wait_ge(turned_out, len(blocks))
            eng.sem_inc(edges_ready, 1)
            bad = eng.value_load(order_bad, min_val=0, max_val=1)

            def tile_tail(t, m, part):
                def after(k):
                    eng.wait_ge(tail, TAIL_N * t + k)
                if part == 0:
                    eng.wait_ge(lin_done, NT + t + 2)
                    eng.wait_ge(resid_in, 16 * t + 16)
                    eng.tensor_tensor(resid[0:m, :], plin[0:m, 0:D], resid[0:m, :], ALU.add).then_inc(tail, 1)
                elif part == 1:
                    after(1)
                    eng.bn_stats(stats[0:m, :], resid[0:m, :]).then_inc(tail, 1)
                    eng.tensor_copy(x1_view(t, m), resid[0:m, :].rearrange("p (a b) -> p a b", a=4)).then_inc(x1_ready, 1)
                elif part == 2:
                    after(2)
                    eng.sem_inc(passed_v, 1)
                    eng.bn_aggr(mv[0:m, :], stats[0:m, :]).then_inc(tail, 1)
                elif part < 3 + RSQRT_N:
                    after(part)
                    rsqrt_step(eng, part - 3, m).then_inc(tail, 1)
                elif part == 3 + RSQRT_N:
                    after(part)
                    eng.wait_ge(x1_ready, t + 2)
                    eng.wait_ge(xf_turned, t + 1)
                    eng.tensor_scalar(hout[0:m, :].rearrange("p (a b) -> p a b", a=4), x1_view(t, m), mv[0:m, 0:1],
                                      rs[0:m, :], ALU.subtract, ALU.mult).then_inc(tail, 1)
                else:
                    after(part)
                    eng.tensor_copy(xf_view(t, m), hout[0:m, :].rearrange("p (a b) -> p a b", a=4)).then_inc(xf_ready, 1)
            TAIL_N = 4 + RSQRT_N
            TAIL_PARTS = 5 + RSQRT_N

            def split_xfT(t, m):
                eng.wait_ge(xf_high, t + 1)
                for h in range(KT):
                    to = xfT[h][:, bass.ds(t, 1), :, 0:m]
                    ins = eng.tensor_tensor(to[:, :, 1, :].rearrange("p a n -> p (a n)"), xft32[:, h, 0:m],
                                            to[:, :, 0, :].rearrange("p a n -> p (a n)"), ALU.subtract)
                ins.then_inc(xfT_ready, 1)

            with eng.If(bad == 0):
                for L in range(2):
                    def one_hot(g, j):
                        eng.tensor_scalar(onehot[j % SR], pattern[:, :], keyT[:, bass.ds(GC * g + j, 1)], None,
                                          ALU.is_equal).then_inc(onehot_ready, 1)

                    def group(g, chunks, clears, end=None):
                        _, base = nc.values_load_multi_w_load_instructions(
                            base_row[0:1, bass.ds(GC * g, GC)], engines=[DVE_ENGINE], min_val=0, max_val=BASE_MAX,
                            skip_runtime_bounds_check_because="a destination node is below N, and a window from there "
                            "ends inside agg")
                        eng.wait_ge(cleared, L * (NT - AHEAD + 1) + clears)
                        part = 0
                        for j in range(chunks):
                            if chunks == GC or j + SR - 1 < chunks:
                                one_hot(g, j + SR - 1)
                            c = L * NCH + GC * g + j
                            eng.wait_ge(chunk_mm, MM_CREDIT + c + 1)
                            eng.wait_ge(chunk_add, ADD_CREDIT + c)
                            to = agg[:, :, :, bass.ds(base[j], WIN)]
                            eng.tensor_tensor(to, to, pchunk[j % SR][:, 0:KT * P].rearrange(
                                "p (h r n) -> p h r n", h=KT, r=R), ALU.add).then_inc(chunk_add, 1)
                            if L == 1 and end is not None:
                                for _ in range(2):
                                    if part < TAIL_PARTS:
                                        tile_tail(end, TN, part)
                                    part += 1
                                if j == 12:
                                    split_xfT(end, TN)

                    for j in range(SR - 1):
                        one_hot(0, j)
                    group(0, GC, 1)
                    group(1, GC, 2)
                    with eng.Fori(2, NT - AHEAD) as g:
                        group(g, GC, g + 1, end=g - 2)
                    for g in range(NT - AHEAD, NG):
                        group(g, GC, NT - AHEAD + 1, end=g - 2)
                    group(NG, CREST, NT - AHEAD + 1, end=NT - 3)
                    if L == 1:
                        for t, m in ((NT - 2, TN), (NT - 1, TLAST)):
                            for part in range(TAIL_PARTS):
                                tile_tail(t, m, part)
                            split_xfT(t, m)
            with eng.Else():
                eng.wait_ge(cleared, 1)
                eng.memset(agg[:, :, :, :], 0.0).then_inc(gen_clear, 1)
                eng.wait_ge(gen_clear, 1)
                for L in range(2):
                    with eng.Fori(0, NCH) as c:
                        eng.wait_ge(gen_key[L], (PASSES + 1) * c + 1)
                        eng.wait_ge(gen_win[L], (PASSES + 1) * c + 1)
                        eng.sem_inc(passed_v, 1)
                        eng.tensor_copy(key_now, keyT[:, bass.ds(c, 1)]).then_inc(gen_key[L], 1)
                        eng.tensor_copy(base_now, base_row[0:1, bass.ds(c, 1)]).then_inc(gen_win[L], 1)
                        with eng.Fori(0, PASSES) as k:
                            n = PASSES * c + k
                            eng.wait_ge(gen_key[L], n + c + 2)
                            eng.wait_ge(gen_win[L], n + c + 2)
                            eng.wait_ge(gen_mm[L], n + 1)
                            eng.sem_inc(passed_v, 1)
                            base = eng.value_load(base_now, min_val=0, max_val=BASE_MAX)
                            eng.tensor_scalar(onehot[0], pattern[:, :], key_now, None,
                                              ALU.is_equal).then_inc(gen_hot[L], 1)
                            eng.wait_ge(gen_mm[L], n + 2)
                            eng.wait_ge(gen_add[L], n + 1)
                            to = agg[:, :, :, bass.ds(base, WIN)]
                            eng.tensor_tensor(to, to, pchunk[0][:, 0:KT * P].rearrange(
                                "p (h r n) -> p h r n", h=KT, r=R), ALU.add).then_inc(gen_add[L], 1)
                            eng.tensor_scalar(key_now, key_now, float(WIN * R), None,
                                              ALU.subtract).then_inc(gen_key[L], 1)
                            eng.tensor_scalar(base_now, base_now, float(WIN), float(BASE_MAX), ALU.add,
                                              ALU.min).then_inc(gen_win[L], 1)
                    if L == 0:
                        eng.wait_ge(staged, NT)
                        eng.memset(agg[:, :, :, :], 0.0).then_inc(gen_clear, 1)
                        eng.wait_ge(gen_clear, 2)
                    else:
                        def tile(t, m):
                            for part in range(TAIL_PARTS):
                                tile_tail(t, m, part)
                            split_xfT(t, m)
                        with eng.Fori(0, NT - 1) as t:
                            tile(t, TN)
                        tile(NT - 1, TLAST)

            n = [0]

            def step(ins):
                n[0] += 1
                ins.then_inc(route, 1)
                eng.wait_ge(route, n[0])

            def mark(want):
                assert n[0] == want, (n[0], want)

            def soft(total):
                step(eng.tensor_reduce(r1, ex[:, 0:total], AX.X, ALU.add))
                step(eng.reciprocal(r2, r1))

            eng.wait_ge(xfT_ready, NT + 1)
            step(eng.tensor_reduce(sumc, colsum[:, :, :], AX.X, ALU.add))
            step(eng.tensor_scalar(mean, sumc, 1.0 / N, None, ALU.mult))
            mark(ROUTE_MEAN)
            eng.wait_ge(ffn_const_in, 64)
            eng.wait_ge(route_pe, 1)
            step(eng.tensor_tensor(lg, pmisc[0:1, 0:NE], brow, ALU.add))
            step(eng.tensor_reduce(r1, lg, AX.X, ALU.max))
            step(eng.tensor_scalar(lg, lg, r1, None, ALU.subtract))
            mark(ROUTE_LOGITS)
            eng.wait_ge(route_act, 1)
            soft(NE)
            step(eng.tensor_scalar(ex, ex, r2, None, ALU.mult))
            step(eng.tensor_scalar(lg, ex, float(N), 1e-30, ALU.mult, ALU.max))
            step(eng.reciprocal(lg, lg))
            step(eng.tensor_scalar(lg, lg, CAPACITY, 1.0, ALU.mult, ALU.min))
            step(eng.tensor_tensor(lg, lg, ex, ALU.mult))
            step(eng.tensor_reduce(r1, lg, AX.X, ALU.max))
            step(eng.tensor_scalar(lg, lg, r1, None, ALU.subtract))
            mark(ROUTE_SCALED)
            eng.wait_ge(route_act, 2)
            soft(NE)
            step(eng.tensor_scalar(ex, ex, r2, None, ALU.mult))
            step(eng.max(top, ex))
            step(eng.max_index(top_i, top, ex))
            mark(ROUTE_TOP)
            step(eng.tensor_scalar(lg[:, 0:2], top[:, 0:2], top[:, 0:1], None, ALU.subtract))
            mark(ROUTE_DIFF)
            eng.wait_ge(route_act, 3)
            soft(2)
            step(eng.tensor_scalar(lg[:, 2:4], ex[:, 0:2], r2, None, ALU.mult))
            mark(ROUTE_WEIGHTS)
            eng.wait_ge(route_pe, 2)
            eng.tensor_scalar(wcol, pmisc[:, 0:2], WSCALE, None, ALU.mult).then_inc(wcol_ready, 1)
            for e in range(2):
                eng.wait_ge(w1_ready[e], 1)
                eng.scalar_tensor_tensor(out=w1s[:, e, 1, :, :], in0=w1e[:, e, :, :], scalar=WSCALE,
                                         in1=w1s[:, e, 0, :, :], op0=ALU.mult, op1=ALU.subtract).then_inc(w1_ready[e], 1)
            eng.wait_ge(b1_turned, 1)
            eng.tensor_copy(b1T, ptr[:, 0:2 * FT]).then_inc(b1_ready, 1)
            eng.wait_ge(wcol_ready, 1)
            for e in range(2):
                eng.wait_ge(w2_high, e + 1)
                step(eng.scalar_tensor_tensor(out=w2s[:, e, 1, :, :], in0=w2e[:, e, :, :], scalar=wcol[:, e:e + 1],
                                              in1=w2s[:, e, 0, :, :], op0=ALU.mult, op1=ALU.subtract))
            step(eng.tensor_scalar(b2w[0:1, :], b2rows[0:1, 0, :], wcol[0:1, 0:1], None, ALU.mult))
            eng.scalar_tensor_tensor(out=b2w[0:1, :], in0=b2rows[0:1, 1, :], scalar=wcol[0:1, 1:2],
                                     in1=b2w[0:1, :], op0=ALU.mult, op1=ALU.add).then_inc(w2_ready, 1)

            def finish(t, half, i, bank, m):
                n = [0]

                def step(ins):
                    n[0] += 1
                    ins.then_inc(fin, 1)
                    eng.wait_ge(fin, FIN_N * t + n[0])
                z = zrow[i][0:m, :]
                z4 = z.rearrange("p (a b) -> p a b", a=4)
                eng.wait_ge(down_done, t + 1)
                eng.wait_ge(o_out[i], 16 * half + 16)
                eng.scalar_tensor_tensor(out=z4, in0=bank[0:m, 0:D].rearrange("p (a b) -> p a b", a=4),
                                         scalar=1.0 / WSCALE, in1=xf_view(t, m), op0=ALU.mult,
                                         op1=ALU.add).then_inc(y_read, 1)
                eng.wait_ge(y_read, t + 5)
                step(eng.bn_stats(stats[0:m, :], z))
                eng.sem_inc(passed_v, 1)
                step(eng.bn_aggr(mv[0:m, :], stats[0:m, :]))
                for k in range(RSQRT_N):
                    step(rsqrt_step(eng, k, m))
                step(eng.tensor_scalar(z, z, mv[0:m, 0:1], rs[0:m, :], ALU.subtract, ALU.mult))
                step(eng.tensor_tensor(z, z, gam[0:m, :], ALU.mult))
                step(eng.tensor_tensor(z, z, bet[0:m, :], ALU.add))
                eng.tensor_tensor(z4, z4, x1_view(t, m), ALU.add).then_inc(o_ready, 1)
                assert n[0] == FIN_N
            FIN_N = 5 + RSQRT_N
            ybank = [plin, ptr, pxf, pmisc]
            with eng.Fori(0, FGROUPS) as q:
                for i in range(4):
                    finish(4 * q + i, 2 * q + i // 2, i % 2, ybank[i], TN)
            finish(NT - 1, (NT - 1) // 2, 0, ybank[0], TLAST)


ROUTE_MEAN = 2
ROUTE_LOGITS = 5
ROUTE_SCALED = 14
ROUTE_TOP = 19
ROUTE_DIFF = 20
ROUTE_WEIGHTS = 23


_INS = ["x", "src", "dst", "edge_type_8", "L0_gnn_W1", "L0_gnn_self_w1", "L0_gnn_b1", "L0_gnn_W2", "L0_gnn_self_w2",
        "L0_gnn_b2", "L0_ffn_Wr", "L0_ffn_br", "L0_ffn_W1", "L0_ffn_b1", "L0_ffn_W2", "L0_ffn_b2", "L0_ffn_gamma",
        "L0_ffn_beta"]


def kernel(**inputs):
    import concourse.bacc as bacc
    from concourse.bass_utils import run_bass_kernel_spmd

    nc = bacc.Bacc("TRN2", target_bir_lowering=False, num_devices=1)
    arrays, ap = {}, {}
    for name in _INS:
        a = np.ascontiguousarray(inputs[name])
        arrays["in_" + name] = a
        ap[name] = nc.dram_tensor("in_" + name, a.shape, mybir.dt.from_np(a.dtype), kind="ExternalInput").ap()
    out = nc.dram_tensor("out_rows", (N, D), F32, kind="ExternalOutput").ap()
    program(nc, ap["x"], ap["src"], ap["dst"], ap["edge_type_8"], [ap["L0_gnn_W1"], ap["L0_gnn_W2"]],
            [ap["L0_gnn_self_w1"], ap["L0_gnn_self_w2"]], [ap["L0_gnn_b1"], ap["L0_gnn_b2"]], ap["L0_ffn_Wr"],
            ap["L0_ffn_br"], ap["L0_ffn_W1"], ap["L0_ffn_b1"], ap["L0_ffn_W2"], ap["L0_ffn_b2"], ap["L0_ffn_gamma"],
            ap["L0_ffn_beta"], out)
    result = run_bass_kernel_spmd(nc, [arrays], core_ids=[0])
    return result.results[0]["out_rows"]
```

```python
from contextlib import ExitStack

import numpy as np

import concourse.bass as bass
from concourse import mybir

F32 = mybir.dt.float32
I32 = mybir.dt.int32
F16 = mybir.dt.float16
U32 = mybir.dt.uint32
ALU = mybir.AluOpType
ACT = mybir.ActivationFunctionType
AX = mybir.AxisListType
DVE_ENGINE = mybir.EngineType.DVE

P = 128
N, D, R, E = 2500, 256, 8, 42500
F, NE = 512, 8
LN_EPS = 1e-5
CAPACITY = float(-(-N * 5 // (4 * NE)))

EC = 128
NCH = -(-E // EC)
CFULL = E // EC
CLAST = E - CFULL * EC
ROWS = -(-NCH // P)
CTAIL = NCH - (ROWS - 1) * P
NEWTON = [1.0, -0.5, 0.0625, -0.5 * 0.0625 ** 3]
RSQRT_N = 10
TAIL_N = 4 + RSQRT_N
TAIL_PARTS = 5 + RSQRT_N
RSQRT_STEPS = 12
TN = 125
NT = N // TN
assert NT * TN == N
WIN = 12
SC = R * WIN
NCOL = N + WIN
GC = 16
NG = NCH // GC
CREST = NCH - NG * GC
AHEAD = 3
LAG = 2
LIN = (3, GC)
GR = 8
SR = 4
NHALF = 2 * NG + 2
PASSES = -(-N // WIN)
GEN_PARTS = [(0, NCH // 2), (NCH // 2, NCH)]
BASE_MAX = NCOL - WIN
MM_CREDIT = 16
ADD_CREDIT = SR
INVALID = 65536.0
RSQRT_MAGIC = float(0x5F3759DF)
KT = D // P
FT = F // P
FH = F // 2
WSCALE = 64.0
FG = 4 * TN
HR = 4
FGROUPS = N // FG
assert FGROUPS * FG == N and FGROUPS % 2 == 1


def ready_chunks(t):
    return GC * (t + LAG)


def slot_uses(slot):
    return (NCH - slot + GR - 1) // GR


def program(nc, x, src, dst, etype, gW, gS, gB, Wr, br, W1, b1, W2, b2, gamma, beta, out):
    lnx = nc.dram_tensor("lnx", [N, D], F32, kind="Internal").ap()
    h1 = nc.dram_tensor("h1", [N, D], F32, kind="Internal").ap()
    table = [lnx, h1]

    ctx = ExitStack()
    with ctx:
        def sb(name, shape, dt=F32):
            return ctx.enter_context(nc.sbuf_tensor(name, shape, dt))

        def sem(name):
            return ctx.enter_context(nc.semaphore(name))

        agg = sb("agg", [P, KT, R, NCOL])
        bulk = sb("bulk", [P, KT * (R + 1) + 3, D])
        W = bulk[:, 0:KT * (R + 1), :]
        hout = bulk[:, KT * (R + 1), :]
        resid = bulk[:, KT * (R + 1) + 1, :]
        selfrow = bulk[:, KT * (R + 1) + 2, :]
        ring = sb("ring", [P, GR * D + SR * SC])
        gath = [ring[:, i * D:(i + 1) * D] for i in range(GR)]
        onehot = [ring[:, GR * D + i * SC:GR * D + (i + 1) * SC] for i in range(SR)]
        edge_i = ring[:, 0:3 * ROWS * P].bitcast(I32).rearrange("p (a j e) -> p a j e", a=3, j=ROWS)
        stage = sb("stage", [P, KT * R, TN])
        edge_f = stage[:, :, :].rearrange("p k n -> p (k n)")[:, 0:3 * ROWS * P].rearrange(
            "p (a j e) -> p a j e", a=3, j=ROWS)
        selfT = sb("selfT", [P, KT, TN])
        xft32 = sb("xft32", [P, KT, TN])
        keyT = sb("keyT", [P, NCH])
        idx = sb("idx", [P, NCH], I32)
        idx_slot = sb("idx_slot", [P, 2 * GR], I32)
        base_row = sb("base_row", [1, ROWS * P], I32)
        ident = sb("ident", [P, P])
        pattern = sb("pattern", [P, SC])
        pattern_i = sb("pattern_i", [P, SC], I32)
        ones = sb("ones", [1, P])
        gbias = sb("gbias", [1, D])
        bet = sb("bet", [P, D])[:, :]
        small = sb("small", [P, 128])
        colsum = sb("colsum", [P, KT, NT])

        pchunk = [ctx.enter_context(nc.psum_tensor(f"pchunk{i}", [P, 512], F32)) for i in range(SR)]
        plin = ctx.enter_context(nc.psum_tensor("plin", [P, 512], F32))
        ptr = ctx.enter_context(nc.psum_tensor("ptr", [P, 512], F32))
        pxf = ctx.enter_context(nc.psum_tensor("pxf", [P, 512], F32))
        pmisc = ctx.enter_context(nc.psum_tensor("pmisc", [P, 512], F32))

        edges_in = [sem(f"edges_in{a}") for a in range(3)]
        x_in = [sem(f"x_in{i}") for i in range(3)]
        consts = sem("consts")
        consts_v = sem("consts_v")
        edge_clear = sem("edge_clear")
        cleared = sem("cleared")
        lists_f = sem("lists_f")
        base_ready = sem("base_ready")
        checks = sem("checks")
        keys = sem("keys")
        ln_stat = sem("ln_stat")
        pro = sem("pro")
        rows_ready = sem("rows_ready")
        check_ready = sem("check_ready")
        rows_turned = sem("rows_turned")
        turned_out = sem("turned_out")
        edges_ready = sem("edges_ready")
        ln_ready = sem("ln_ready")
        ln_ready_v = sem("ln_ready_v")
        ln_stats_in = sem("ln_stats_in")
        lnx_out = sem("lnx_out")
        w_in = sem("w_in")
        idx_ready = sem("idx_ready")
        gathered = [sem(f"gathered{i}") for i in range(GR)]
        onehot_ready = sem("onehot_ready")
        chunk_mm = sem("chunk_mm")
        chunk_add = sem("chunk_add")
        self_in = sem("self_in")
        self_turned = sem("self_turned")
        selfT_ready = sem("selfT_ready")
        staged = sem("staged")
        lin_done = sem("lin_done")
        h_ready = sem("h_ready")
        h_out = sem("h_out")
        resid_in = sem("resid_in")
        x1_ready = sem("x1_ready")
        tail = sem("tail")
        xf_ready = sem("xf_ready")
        xf_turned = sem("xf_turned")
        xfT_ready = sem("xfT_ready")
        gen_idx = sem("gen_idx")
        gen_in = sem("gen_in")
        gen_hot = [sem(f"gen_hot{i}") for i in range(4)]
        gen_mm = [sem(f"gen_mm{i}") for i in range(4)]
        gen_add = [sem(f"gen_add{i}") for i in range(4)]
        gen_win = [sem(f"gen_win{i}") for i in range(4)]
        gen_key = [sem(f"gen_key{i}") for i in range(4)]
        gen_clear = sem("gen_clear")
        route = sem("route")
        route_pe = sem("route_pe")
        route_act = sem("route_act")
        ffn_const_in = sem("ffn_const_in")
        expert_in = [sem(f"expert_in{b}") for b in range(4)]
        b1_in = sem("b1_in")
        expert_rest = sem("expert_rest")
        w2_ready = sem("w2_ready")
        b1_turned = sem("b1_turned")
        b1_ready = sem("b1_ready")
        up_done = sem("up_done")
        gelu_done = sem("gelu_done")
        down_done = sem("down_done")
        w1_ready = [sem(f"w1_ready{b}") for b in range(4)]
        wcol_ready = sem("wcol_ready")
        high_ready = sem("high_ready")
        low_ready = sem("low_ready")
        xf_high = sem("xf_high")
        y_read = sem("y_read")
        fin = sem("fin")
        o_ready = sem("o_ready")
        o_out = [sem(f"o_out{i}") for i in range(4)]
        beta_in = sem("beta_in")
        bias_added = sem("bias_added")
        beta_added = sem("beta_added")

        key_now = small[:, 124:125]
        base_now = small[0:1, 125:126].bitcast(I32)
        passed = sem("passed")
        passed_v = sem("passed_v")
        passed_p = sem("passed_p")

        stats = small[:, 0:6]
        mv = small[:, 6:8]
        rs = small[:, 8:9]
        rs_var = small[:, 9:10]
        rs_tmp = small[:, 10:11]
        emin = small[:, 12:12 + ROWS]
        emax = small[:, 16:16 + ROWS]
        echk = small[:, 20:20 + ROWS]
        ebound = small[:, 24:24 + ROWS]
        ebound_i = small[:, 28:28 + ROWS].bitcast(I32)
        eupper = small[:, 84:84 + ROWS]
        eupper_i = small[:, 92:92 + ROWS].bitcast(I32)
        order_bad = small[0:1, 33:34].bitcast(I32)
        wcol = small[:, 40:42]
        b1T = small[:, 48:48 + 2 * FT]
        lg = small[0:1, 56:64]
        ex = small[0:1, 64:72]
        top = small[0:1, 72:80]
        top_i = small[0:1, 80:88].bitcast(U32)
        r1 = small[0:1, 88:89]
        r2 = small[0:1, 89:90]
        rsum = small[0:1, 90:91]
        zero = small[:, 126:127].rearrange("p (a b) -> p a b", a=1)
        brow = small[0:1, 96:104]
        sumc = small[:, 104:104 + KT]
        WrT = small[:, 108:108 + KT * NE].rearrange("p (k e) -> p k e", k=KT)

        def x1_view(t, m):
            return agg[0:m, 0, 0:4, bass.ds(TN * t, 64)]

        def xf_view(t, m):
            return agg[0:m, 0, 4:8, bass.ds(TN * t, 64)]

        xfT = [agg[:, 1, h, 0:N].bitcast(F16).rearrange("p (t s n) -> p t s n", s=2, n=TN) for h in range(KT)]
        late = agg[:, 1, KT:R, :].rearrange("p r n -> p (r n)")
        at = 0

        def carve(cols):
            nonlocal at
            at += cols
            assert at <= (R - KT) * NCOL
            return late[:, at - cols:at]
        w1s = carve(2 * KT * F).bitcast(F16).rearrange("p (e s k f) -> p e s k f", e=2, s=2, k=KT)
        w2s = carve(2 * FT * D).bitcast(F16).rearrange("p (e s k d) -> p e s k d", e=2, s=2, k=FT)
        hid = carve(2 * 2 * FT * FG).bitcast(F16).rearrange("p (b k s n) -> p b k s n", b=2, k=2 * FT, s=2)
        flat = bulk[:, :, :].rearrange("p t d -> p (t d)")
        w1e = flat[:, 0:2 * KT * F].rearrange("p (e k f) -> p e k f", e=2, k=KT)
        w2e = flat[:, 2 * KT * F:2 * KT * F + 2 * FT * D].rearrange("p (e k d) -> p e k d", e=2, k=FT)
        g32 = [ring[:, i * FG:(i + 1) * FG] for i in range(HR)]
        gam = carve(D)
        b1rows = carve(P)
        b2rows = carve(2 * D).rearrange("p (e d) -> p e d", e=2)
        b2w = carve(D)
        zrow = [carve(D) for _ in range(4)]

        ln_cols = agg[:, KT - 1, R - 1, N - 12 * NT:N]
        ln_stats = ln_cols[:, 0:6 * NT].rearrange("p (t s) -> p t s", s=6)
        ln_mv = ln_cols[:, 6 * NT:8 * NT].rearrange("p (t s) -> p t s", s=2)
        ln_rs = ln_cols[:, 8 * NT:9 * NT]
        ln_var = ln_cols[:, 9 * NT:10 * NT]
        ln_tmp = ln_cols[:, 10 * NT:11 * NT]
        ln_shift = ln_cols[:, 11 * NT:12 * NT]
        fin_stats = keyT[:, 0:24].rearrange("p (t s) -> p t s", s=6)
        fin_mv = keyT[:, 24:32].rearrange("p (t s) -> p t s", s=2)
        fin_cols = keyT[:, 32:44].rearrange("p (k t) -> p k t", t=4)

        def general(eng, L, chunk, windows=()):
            for i, (c0, c1) in enumerate(GEN_PARTS):
                s = len(GEN_PARTS) * L + i
                if i > 0:
                    eng.wait_ge(gen_add[s - 1], PASSES * c0 + 1)
                    for own in windows:
                        eng.wait_ge(own[s - 1], (PASSES + 1) * c0 + 1)
                with eng.Fori(0, c1 - c0) as c:
                    chunk(s, c0, c)

        block = ctx.enter_context(nc.Block())

        def rsqrt_steps(eng, step, y, v, var, tmp):
            yi, vi = y.bitcast(I32), v.bitcast(I32)
            step(eng.tensor_scalar(v, var, LN_EPS, None, ALU.add))
            step(eng.tensor_scalar(yi, vi, 1, None, ALU.arith_shift_right))
            step(eng.tensor_scalar(yi, yi, -1.0, RSQRT_MAGIC, ALU.mult, ALU.add))
            for _ in range(3):
                step(eng.tensor_tensor(tmp, y, y, ALU.mult))
                step(eng.scalar_tensor_tensor(out=tmp, in0=tmp, scalar=-0.5, in1=v, op0=ALU.mult, op1=ALU.mult))
                step(eng.scalar_tensor_tensor(out=y, in0=tmp, scalar=1.5, in1=y, op0=ALU.add, op1=ALU.mult))

        def rsqrt_step(eng, k, m):
            y, v, t = rs[0:m, :], rs_var[0:m, :], rs_tmp[0:m, :]
            if k == 0:
                return eng.tensor_scalar(v, mv[0:m, 1:2], LN_EPS, None, ALU.add)
            if k == 1:
                return eng.tensor_scalar(y.bitcast(I32), v.bitcast(I32), 1, None, ALU.arith_shift_right)
            if k == 2:
                return eng.tensor_scalar(y.bitcast(I32), y.bitcast(I32), -1.0, RSQRT_MAGIC, ALU.mult, ALU.add)
            if k == RSQRT_N - 1:
                return eng.tensor_scalar(y, y, NEWTON[3], None, ALU.mult)
            a = NEWTON[(k - 3) // 2]
            if k % 2:
                return eng.scalar_tensor_tensor(out=t, in0=y, scalar=y, in1=v, op0=ALU.mult, op1=ALU.mult)
            return eng.scalar_tensor_tensor(out=y, in0=t, scalar=3.0 / (a * a), in1=y, op0=ALU.subtract, op1=ALU.mult)

        XB = [(0, 7), (7, 14), (14, NT)]
        XACT = 17

        def load_x(eng, b):
            t0, t1 = XB[b]
            eng.dma_start(bulk[0:TN, t0:t1, :],
                          x[t0 * TN:t1 * TN, :].rearrange("(t p) d -> p t d", p=TN)).then_inc(x_in[b], 16)

        @block.sync
        def _(eng):
            lists = (dst, etype, src)
            full = (ROWS - 1) * P * EC
            for a, lst in enumerate(lists):
                eng.dma_start(edge_i[:, a, 0:ROWS - 1, :],
                              lst[0:full].rearrange("(j p e) -> p j e", p=P, e=EC)).then_inc(edges_in[a], 16)
            eng.wait_ge(edge_clear, 1)
            for a, lst in enumerate(lists):
                eng.dma_start(edge_i[0:CTAIL - 1, a, ROWS - 1, :],
                              lst[full:CFULL * EC].rearrange("(p e) -> p e", e=EC)).then_inc(edges_in[a], 16)
                if a == 0:
                    eng.dma_start(edge_i[CTAIL - 1:CTAIL, a, ROWS - 1, :],
                                  lst[E - EC:E].rearrange("(p e) -> p e", p=1)).then_inc(edges_in[a], 16)
                else:
                    eng.dma_start(edge_i[CTAIL - 1:CTAIL, a, ROWS - 1, EC - CLAST:EC],
                                  lst[E - CLAST:E].rearrange("(p e) -> p e", p=1)).then_inc(edges_in[a], 16)
                if a == 1:
                    load_x(eng, 2)
            for b, (t0, t1) in enumerate(XB):
                eng.wait_ge(ln_ready, b + 1)
                if t1 == NT:
                    eng.wait_ge(ln_ready_v, 1)
                eng.dma_start(lnx[t0 * TN:t1 * TN, :].rearrange("(t p) d -> p t d", p=TN),
                              bulk[0:TN, t0:t1, :]).then_inc(lnx_out, 16)

            def load_weights(L):
                eng.dma_start(W[:, 0:KT * R, :], gW[L].rearrange("r (h p) o -> p (r h) o", p=P)).then_inc(w_in, 16)
                eng.dma_start(W[:, KT * R:, :], gS[L].rearrange("(h p) o -> p h o", p=P)).then_inc(w_in, 16)
                eng.dma_start(gbias[:, :], gB[L].rearrange("(a d) -> a d", a=1)).then_inc(w_in, 16)

            def load_rows(L, t, m):
                T = L * NT + t
                eng.wait_ge(self_turned, T + 1)
                eng.dma_start(selfrow[0:m, :], table[L][bass.ds(TN * t, m), :]).then_inc(self_in, 16)
                if L == 1:
                    eng.wait_ge(x1_ready, t + 1)
                    eng.dma_start(resid[0:m, :], x[bass.ds(TN * t, m), :]).then_inc(resid_in, 16)

            def store_h(t, m):
                eng.wait_ge(h_ready, t + 2)
                eng.dma_start(h1[bass.ds(TN * t, m), :], hout[0:m, :]).then_inc(h_out, 16)

            eng.dma_start(bet, beta.rearrange("(a d) -> a d", a=1).to_broadcast([P, D])).then_inc(beta_in, 16)
            for L in range(2):
                if L == 0:
                    eng.wait_ge(lnx_out, 48)
                else:
                    eng.wait_ge(h_out, 16 * NT + 16)
                    eng.wait_ge(lin_done, NT + 1)
                load_weights(L)
                load_rows(L, 0, TN)
                with eng.Fori(0, NT - 2) as t:
                    load_rows(L, t + 1, TN)
                    if L == 0:
                        store_h(t, TN)
                load_rows(L, NT - 1, TN)
                if L == 0:
                    store_h(NT - 2, TN)
                    store_h(NT - 1, TN)
            eng.dma_start(WrT, Wr.rearrange("(k p) e -> p k e", p=P)).then_inc(ffn_const_in, 16)
            eng.dma_start(brow, br.rearrange("(a e) -> a e", a=1)).then_inc(ffn_const_in, 16)
            eng.wait_ge(lin_done, 2 * NT + 1)
            eng.dma_start(gam, gamma.rearrange("(a d) -> a d", a=1).to_broadcast([P, D])).then_inc(ffn_const_in, 16)
            eng.wait_ge(route, ROUTE_TOP)
            ex_i = [eng.value_load(top_i[0:1, k:k + 1], min_val=0, max_val=NE - 1) for k in range(2)]
            for k, e in enumerate(ex_i):
                if k == 1:
                    for i, ei in enumerate(ex_i):
                        eng.dma_start(b1rows[FT * i:FT * (i + 1), :],
                                      b1[bass.ds(ei, 1), :].rearrange("a (k p) -> (a k) p", p=P)).then_inc(b1_in, 16)
                for b in range(2):
                    eng.dma_start(w1e[:, k, :, b * FH:(b + 1) * FH], W1[bass.ds(e, 1), :, b * FH:(b + 1) * FH].rearrange(
                        "a (k p) f -> p (a k) f", p=P)).then_inc(expert_in[2 * k + b], 16)
            for k, e in enumerate(ex_i):
                eng.dma_start(w2e[:, k, :, :],
                              W2[bass.ds(e, 1), :, :].rearrange("a (k p) d -> p (a k) d", p=P)).then_inc(expert_rest, 16)
                eng.dma_start(b2rows[:, k, :], b2[bass.ds(e, 1), :].to_broadcast([P, D])).then_inc(expert_rest, 16)
            with eng.Fori(0, FGROUPS) as q:
                for i in range(4):
                    eng.wait_ge(o_ready, 4 * q + i + 1)
                    eng.dma_start(out[bass.ds(TN * (4 * q + i), TN), :], zrow[i][0:TN, :]).then_inc(o_out[i], 16)
            for i in range(4):
                eng.wait_ge(o_out[i], 16 * FGROUPS + 16)

        def order_check(eng):
            n = [0]

            def step(ins):
                n[0] += 1
                ins.then_inc(checks, 1)
                eng.wait_ge(checks, n[0])
            eng.tensor_tensor(ebound, ebound, emin, ALU.subtract)
            eng.tensor_tensor(eupper, emin, eupper, ALU.subtract)
            step(eng.tensor_tensor(emax, emax, emin, ALU.subtract))
            eng.tensor_scalar(ebound, ebound, 0.0, None, ALU.max)
            eng.tensor_scalar(eupper, eupper, 0.0, None, ALU.max)
            step(eng.tensor_scalar(emax, emax, float(WIN - 1), 0.0, ALU.subtract, ALU.max))
            step(eng.tensor_tensor(emax, emax, ebound, ALU.add))
            for j in range(ROWS):
                m = P if j < ROWS - 1 else CTAIL
                ins = eng.tensor_tensor(echk[0:m, j:j + 1], emax[0:m, j:j + 1], eupper[0:m, j:j + 1], ALU.add)
            step(ins)
            for j in range(1, ROWS):
                step(eng.tensor_tensor(echk[:, 0:1], echk[:, 0:1], echk[:, j:j + 1], ALU.add))
            eng.sem_inc(check_ready, 1)

        @block.gpsimd
        def _(eng):
            eng.memset(ident[:, :], 0.0).then_inc(consts, 1)
            eng.iota(pattern_i[:, :], pattern=[[1, R], [R, WIN]], base=0, channel_multiplier=0).then_inc(consts, 1)
            eng.iota(ebound_i[:, :], pattern=[[P, ROWS]], base=-GC * (LAG - 1), channel_multiplier=1).then_inc(consts, 1)
            eng.iota(eupper_i[:, :], pattern=[[P, ROWS]], base=0, channel_multiplier=1).then_inc(consts, 1)
            eng.wait_ge(consts, 1)
            eng.affine_select(out=ident[:, :], in_=ident[:, :], compare_op=ALU.not_equal, fill=1.0,
                              base=0, pattern=[[-1, P]], channel_multiplier=1).then_inc(consts, 1)
            for a in range(3):
                eng.wait_ge(edges_in[a], 48)
                eng.tensor_copy(edge_f[:, a, :, :], edge_i[:, a, :, :]).then_inc(lists_f, 1)
            eng.wait_ge(base_ready, 1)
            order_check(eng)
            for j in range(ROWS):
                eng.tensor_scalar(edge_f[:, 0, j, :], edge_f[:, 0, j, :], emin[:, j:j + 1], float(R),
                                  ALU.subtract, ALU.mult).then_inc(keys, 1)
            eng.wait_ge(keys, ROWS)
            eng.tensor_tensor(edge_f[:, 1, :, :], edge_f[:, 1, :, :], edge_f[:, 0, :, :],
                              ALU.add).then_inc(rows_ready, 1)
            eng.wait_ge(edges_ready, 1)
            bad = eng.value_load(order_bad, min_val=0, max_val=1)
            with eng.If(bad == 0):
                for L in range(2):
                    def gather(g, j):
                        s = j % GR
                        eng.wait_ge(idx_ready, L * NHALF + 2 * g + j // GR + 1)
                        eng.wait_ge(chunk_mm, MM_CREDIT + L * NCH + GC * g + j - GR + 1)
                        eng.sem_inc(passed, 1)
                        eng.indirect_dma_start(out=gath[s], out_offset=None, in_=table[L][:, :],
                                               in_offset=bass.IndirectOffsetOnAxis(
                                                   ap=idx_slot[:, j:j + 1], axis=0)).then_inc(gathered[s], 16)
                    if L == 0:
                        eng.wait_ge(lnx_out, 48)
                    else:
                        eng.wait_ge(h_out, 16 * NT + 16)
                    with eng.Fori(0, NG) as g:
                        for j in range(GC):
                            gather(g, j)
                    for j in range(CREST):
                        gather(NG, j)
            with eng.Else():
                for L in range(2):
                    if L == 0:
                        eng.wait_ge(lnx_out, 48)
                    else:
                        eng.wait_ge(h_out, 16 * NT + 16)

                    def chunk(s, c0, c):
                        eng.wait_ge(gen_mm[s], PASSES * c + 1)
                        eng.tensor_copy(idx_slot[:, 0:1], idx[:, bass.ds(c0 + c, 1)]).then_inc(gen_idx, 1)
                        eng.wait_ge(gen_idx, L * NCH + c0 + c + 1)
                        eng.sem_inc(passed, 1)
                        eng.indirect_dma_start(out=gath[0], out_offset=None, in_=table[L][:, :],
                                               in_offset=bass.IndirectOffsetOnAxis(
                                                   ap=idx_slot[:, 0:1], axis=0)).then_inc(gen_in, 16)
                    general(eng, L, chunk)

            def add_beta(t, m):
                x1 = x1_view(t, m)
                eng.wait_ge(xf_ready, t + 1)
                eng.sem_inc(passed, 1)
                eng.tensor_tensor(x1, x1, bet[0:m, :].rearrange("p (a b) -> p a b", a=4), ALU.add).then_inc(beta_added, 1)
            eng.wait_ge(beta_in, 16)
            with eng.Fori(0, NT - 1) as t:
                add_beta(t, TN)
            add_beta(NT - 1, TN)

            def lows(q, buf, m):
                for k in range(2 * FT):
                    eng.wait_ge(high_ready, 2 * FT * q + k + 1)
                    eng.tensor_tensor(hid[:, buf, k, 1, 0:m], g32[k % HR][:, 0:m], hid[:, buf, k, 0, 0:m],
                                      ALU.subtract).then_inc(low_ready, 1)
            lows(0, 0, FG)
            with eng.Fori(0, (FGROUPS - 1) // 2) as u:
                lows(2 * u + 1, 1, FG)
                lows(2 * u + 2, 0, FG)

        @block.scalar
        def _(eng):
            load_x(eng, 0)
            load_x(eng, 1)
            eng.wait_ge(consts_v, 1)
            eng.activation(agg[:, :, :, N:NCOL].rearrange("p h r n -> p (h r) n"),
                           zero.to_broadcast([P, KT * R, WIN]), ACT.Copy)
            eng.activation(agg[:, :, :, 0:AHEAD * TN].rearrange("p h r n -> p (h r) n"),
                           zero.to_broadcast([P, KT * R, AHEAD * TN]), ACT.Copy).then_inc(cleared, 1)
            for b, (t0, t1) in enumerate(XB):
                eng.wait_ge(ln_stat, b + 1)
                for t in range(t0, min(t1, XACT)):
                    m = TN
                    ins = eng.activation(bulk[0:m, t, :], bulk[0:m, t, :], ACT.Identity, bias=ln_shift[0:m, t:t + 1],
                                         scale=ln_rs[0:m, t:t + 1])
                ins.then_inc(ln_ready, 1)

            def turn_self(L, t, m):
                T = L * NT + t
                eng.wait_ge(self_turned, T + 2)
                eng.wait_ge(lin_done, T + 1)
                eng.activation(selfT[:, :, 0:m], ptr[:, 0:KT * m].rearrange("p (k n) -> p k n", k=KT),
                               ACT.Copy).then_inc(selfT_ready, 1)

            def stage_tile(L, t, m):
                T = L * NT + t
                eng.wait_ge(lin_done, T + 1)
                for h in range(KT):
                    eng.activation(stage[:, h * R:(h + 1) * R, 0:m], agg[:, h, :, bass.ds(TN * t, m)],
                                   ACT.Copy).then_inc(staged, 1)

            def relu_rows(t, m):
                eng.wait_ge(lin_done, t + 2)
                eng.wait_ge(h_out, 16 * t + 16)
                eng.activation(hout[0:m, :], plin[0:m, 0:D], ACT.Relu).then_inc(h_ready, 1)

            def keep_xfT(t, m):
                eng.wait_ge(xf_turned, t + 2)
                eng.wait_ge(xfT_ready, t + 1)
                for h in range(KT):
                    eng.activation(xft32[:, h, 0:m], pxf[:, h * TN:h * TN + m], ACT.Identity,
                                   accum_out=colsum[:, h, bass.ds(t, 1)])
                for h in range(KT):
                    ins = eng.activation(xfT[h][:, bass.ds(t, 1), 0, 0:m].rearrange("p a n -> p (a n)"),
                                         pxf[:, h * TN:h * TN + m], ACT.Copy)
                ins.then_inc(xf_high, 1)

            def clear_columns(t, tiles):
                eng.activation(agg[:, :, :, bass.ds(TN * t, TN * tiles)].rearrange("p h r n -> p (h r) n"),
                               zero.to_broadcast([P, KT * R, TN * tiles]), ACT.Copy).then_inc(cleared, 1)

            def copy_indices(L, half, c0, cols):
                eng.wait_ge(chunk_mm, MM_CREDIT + L * NCH + c0 - GR)
                eng.activation(idx_slot[:, half * GR:half * GR + cols], idx[:, bass.ds(c0, cols)],
                               ACT.Copy).then_inc(idx_ready, 1)

            eng.wait_ge(edges_ready, 1)
            bad = eng.value_load(order_bad, min_val=0, max_val=1)
            with eng.If(bad == 0):
                for L in range(2):
                    def group(g, lin=None, end=None, clear=False, copies=(GR, GR), first=False):
                        if lin is not None:
                            turn_self(L, lin, TN)
                            eng.wait_ge(chunk_add, ADD_CREDIT + L * NCH + ready_chunks(lin))
                            stage_tile(L, lin, TN)
                        if copies:
                            copy_indices(L, 0, GC * g + GC, copies[0])
                        if clear:
                            clear_columns(g + AHEAD, 1)
                        if first:
                            clear_columns(0, AHEAD)
                        if L == 1 and end is not None:
                            keep_xfT(end, TN)
                        if L == 0 and lin is not None:
                            relu_rows(lin, TN)
                        if copies:
                            copy_indices(L, 1, GC * g + GC + GR, copies[1])

                    if L == 1:
                        eng.wait_ge(chunk_mm, MM_CREDIT + NCH)
                    copy_indices(L, 0, 0, GR)
                    copy_indices(L, 1, GR, GR)
                    group(0, clear=True)
                    group(1, clear=True)
                    group(2, lin=0, clear=True)
                    with eng.Fori(3, NT - AHEAD) as g:
                        group(g, lin=g - LAG, end=g - LAG - 1, clear=True)
                    for g in range(NT - AHEAD, NG - 1):
                        group(g, lin=g - LAG, end=g - LAG - 1)
                    group(NG - 1, lin=NT - 3, end=NT - 4, copies=(GR, CREST - GR))
                    group(NG, lin=NT - 2, end=NT - 3, copies=None, first=(L == 0))
                    turn_self(L, NT - 1, TN)
                    eng.wait_ge(chunk_add, ADD_CREDIT + L * NCH + NCH)
                    stage_tile(L, NT - 1, TN)
                    if L == 0:
                        relu_rows(NT - 1, TN)
                    else:
                        keep_xfT(NT - 2, TN)
                        keep_xfT(NT - 1, TN)
            with eng.Else():
                for L in range(2):
                    eng.wait_ge(gen_add[2 * L + 1], PASSES * (NCH - GEN_PARTS[1][0]) + 1)

                    def tile(t, m):
                        turn_self(L, t, m)
                        stage_tile(L, t, m)
                        if L == 0:
                            relu_rows(t, m)
                        else:
                            keep_xfT(t, m)
                    with eng.Fori(0, NT - 1) as t:
                        tile(t, TN)
                    tile(NT - 1, TN)
            eng.wait_ge(route, ROUTE_LOGITS)
            eng.activation(ex, lg, ACT.Exp, accum_out=rsum).then_inc(route_act, 1)
            eng.wait_ge(route, ROUTE_SCALED)
            eng.activation(ex, lg, ACT.Exp, accum_out=rsum).then_inc(route_act, 1)
            eng.wait_ge(route, ROUTE_DIFF)
            eng.activation(ex[:, 0:2], lg[:, 0:2], ACT.Exp, accum_out=rsum).then_inc(route_act, 1)
            eng.wait_ge(route_act, 3)
            eng.activation(r1, zero[0:1, :, 0], ACT.Gelu).then_inc(route_act, 1)
            for b in range(4):
                e, cols = b // 2, slice(b % 2 * FH, (b % 2 + 1) * FH)
                eng.wait_ge(expert_in[b], 16)
                eng.activation(w1s[:, e, 0, :, cols], w1e[:, e, :, cols], ACT.Copy, scale=WSCALE).then_inc(w1_ready[b], 1)
            eng.wait_ge(b1_ready, 1)

            def gelu(q, buf, m):
                for k in range(2 * FT):
                    eng.wait_ge(up_done, 2 * FT * q + k + 1)
                    eng.wait_ge(low_ready, 2 * FT * q + k + 1)
                    eng.activation(g32[k % HR][:, 0:m], pchunk[k % SR][:, 0:m], ACT.Gelu, bias=b1T[:, k:k + 1],
                                   scale=1.0 / WSCALE).then_inc(gelu_done, 1)
                    eng.wait_ge(gelu_done, SR + 2 * FT * q + k + 1)
                    eng.activation(hid[:, buf, k, 0, 0:m], g32[k % HR][:, 0:m], ACT.Copy).then_inc(high_ready, 1)
            gelu(0, 0, FG)
            with eng.Fori(0, (FGROUPS - 1) // 2) as u:
                gelu(2 * u + 1, 1, FG)
                gelu(2 * u + 2, 0, FG)

        @block.tensor
        def _(eng):
            eng.wait_ge(consts, 5)
            eng.wait_ge(rows_ready, 1)
            blocks = [(a, j) for a in range(2) for j in range(ROWS)]
            for n, (a, j) in enumerate(blocks):
                m = P if j < ROWS - 1 else CTAIL
                if n >= SR:
                    eng.wait_ge(turned_out, n - SR + 1)
                eng.transpose(pchunk[n % SR][:, 0:m], edge_f[0:m, a + 1, j, :], ident[0:m, 0:m]).then_inc(rows_turned, 1)
            for j in range(ROWS):
                ins = eng.transpose(plin[0:1, j * P:(j + 1) * P], emin[:, j:j + 1], ident[:, :])
            ins.then_inc(rows_turned, 1)
            eng.wait_ge(check_ready, 1)
            eng.transpose(ptr[0:1, 0:P], echk[:, 0:1], ident[:, :]).then_inc(rows_turned, 1)
            eng.wait_ge(edges_ready, 1)
            bad = eng.value_load(order_bad, min_val=0, max_val=1)

            def turn_self(L, t, m):
                T = L * NT + t
                eng.wait_ge(self_in, 16 * T + 16)
                eng.wait_ge(selfT_ready, T + 1)
                for h in range(KT):
                    ins = eng.transpose(ptr[:, h * m:(h + 1) * m], selfrow[0:m, h * P:(h + 1) * P], ident[0:m, 0:m])
                ins.then_inc(self_turned, 1)

            def products(L, t, m, k0, k1):
                T = L * NT + t
                for k in range(k0, k1):
                    if k == 0:
                        if L == 0:
                            eng.wait_ge(h_ready, t + 1)
                        else:
                            eng.wait_ge(h_ready, NT + 1)
                            eng.wait_ge(tail, TAIL_N * t + 1)
                        eng.matmul(plin[0:m, 0:D], ones[0:1, 0:m], gbias[0:1, :], start=True, stop=False)
                    elif k <= KT:
                        if k == 1:
                            eng.wait_ge(selfT_ready, T + 2)
                        eng.matmul(plin[0:m, 0:D], selfT[:, k - 1, 0:m], W[:, KT * R + k - 1, :], start=False, stop=False)
                    else:
                        h, r = (k - KT - 1) // R, (k - KT - 1) % R
                        if r == 0:
                            eng.wait_ge(staged, KT * T + h + 1)
                        ins = eng.matmul(plin[0:m, 0:D], stage[:, h * R + r, 0:m], W[:, KT * r + h, :],
                                         start=False, stop=(k == KT * (R + 1)))
                        if k == KT * (R + 1):
                            ins.then_inc(lin_done, 1)
            STEPS = KT * (R + 1) + 1

            def turn_xf(t, m):
                eng.wait_ge(xf_ready, t + 1)
                eng.wait_ge(xfT_ready, t + 1)
                for h in range(KT):
                    ins = eng.transpose(pxf[:, h * TN:h * TN + m], hout[0:m, h * P:(h + 1) * P], ident[0:m, 0:m])
                ins.then_inc(xf_turned, 1)

            with eng.If(bad == 0):
                for L in range(2):
                    def chunk(g, j):
                        s = j % GR
                        first = j // GR + 1 + L * slot_uses(s)
                        eng.wait_ge(gathered[s], 16 * (2 * g + first))
                        eng.wait_ge(onehot_ready, L * NCH + GC * g + j + 1)
                        eng.wait_ge(chunk_add, L * NCH + GC * g + j + 1)
                        for h in range(KT):
                            ins = eng.matmul(pchunk[j % SR][:, h * SC:(h + 1) * SC], gath[s][:, h * P:(h + 1) * P],
                                             onehot[j % SR], start=True, stop=True)
                        ins.then_inc(chunk_mm, 1)

                    def group(g, chunks, lin=None, end=None):
                        for j in range(chunks):
                            chunk(g, j)
                            if j == 10 and L == 1 and end is not None:
                                turn_xf(end, TN)
                            if lin is None:
                                continue
                            if j == 0:
                                turn_self(L, lin, TN)
                            if j == LIN[0] - 1:
                                products(L, lin, TN, 0, KT + 1)
                            if LIN[0] <= j < LIN[1]:
                                done, left = j - LIN[0], min(chunks, LIN[1]) - LIN[0]
                                products(L, lin, TN, KT + 1 + KT * R * done // left, KT + 1 + KT * R * (done + 1) // left)

                    eng.wait_ge(chunk_add, ADD_CREDIT + L * NCH)
                    group(0, GC)
                    group(1, GC)
                    eng.wait_ge(w_in, 48 * (L + 1))
                    group(2, GC, lin=0)
                    with eng.Fori(3, NG) as g:
                        group(g, GC, lin=g - LAG, end=g - LAG - 1)
                    group(NG, CREST, lin=NT - 2, end=NT - 3)
                    turn_self(L, NT - 1, TN)
                    products(L, NT - 1, TN, 0, STEPS)
                    if L == 1:
                        turn_xf(NT - 2, TN)
                        turn_xf(NT - 1, TN)
            with eng.Else():
                for L in range(2):
                    def chunk(s, c0, c):
                        eng.wait_ge(gen_in, 16 * (L * NCH + c0 + c) + 16)
                        eng.sem_inc(passed_p, 1)
                        with eng.Fori(0, PASSES) as k:
                            eng.wait_ge(gen_hot[s], PASSES * c + k + 1)
                            eng.wait_ge(gen_add[s], PASSES * c + k + 1)
                            for h in range(KT):
                                ins = eng.matmul(pchunk[0][:, h * SC:(h + 1) * SC], gath[0][:, h * P:(h + 1) * P],
                                                 onehot[0], start=True, stop=True)
                            ins.then_inc(gen_mm[s], 1)
                    general(eng, L, chunk)
                    eng.wait_ge(w_in, 48 * (L + 1))

                    def tile(t, m):
                        turn_self(L, t, m)
                        products(L, t, m, 0, STEPS)
                        if L == 1:
                            turn_xf(t, m)
                    with eng.Fori(0, NT - 1) as t:
                        tile(t, TN)
                    tile(NT - 1, TN)
            eng.wait_ge(ffn_const_in, 48)
            eng.wait_ge(route, ROUTE_SUMS)
            for k in range(KT):
                ins = eng.matmul(pmisc[0:1, 0:NE], sumc[:, k:k + 1], WrT[:, k, :], start=(k == 0), stop=(k == KT - 1))
            ins.then_inc(route_pe, 1)
            eng.wait_ge(route, ROUTE_WEIGHTS)
            eng.matmul(pmisc[:, 0:2], ones[0:1, :], lg[:, 2:4], start=True, stop=True).then_inc(route_pe, 1)

            ybank = [plin, ptr, pxf, pmisc]

            def up(q, m, first=False):
                for k in range(2 * FT):
                    e, f = k // FT, k % FT
                    if first and f % 2 == 0:
                        eng.wait_ge(w1_ready[k // 2], 2)
                    eng.wait_ge(gelu_done, 2 * FT * q + k + 1)
                    n = 0
                    for sw, sx in ((0, 0), (0, 1), (1, 0)):
                        for i in range(KT):
                            tiles, cols = 4, TN
                            ins = eng.matmul(pchunk[k % SR][:, 0:m].rearrange("p (t n) -> p t n", t=tiles),
                                             w1s[:, e, sw, i, f * P:(f + 1) * P],
                                             xfT[i][:, bass.ds(4 * q, tiles), sx, 0:cols], start=(n == 0), stop=(n == 5))
                            n += 1
                    ins.then_inc(up_done, 1)
                    if first and k == 0:
                        eng.wait_ge(b1_in, 32)
                        eng.transpose(ptr[:, 0:2 * FT], b1rows[0:2 * FT, :], ident[0:2 * FT, 0:2 * FT]).then_inc(b1_turned, 1)

            def down(q, buf, tiles):
                for i, mt in enumerate(tiles):
                    eng.wait_ge(y_read, 4 * q + i + 1)
                    for k in range(2 * FT):
                        if i == 0:
                            eng.wait_ge(low_ready, HR + 2 * FT * q + k + 1)
                        for sh, sw in ((0, 0), (0, 1), (1, 0)):
                            ins = eng.matmul(ybank[i][0:mt, 0:D], hid[:, buf, k, sh, i * TN:i * TN + mt],
                                             w2s[:, k // FT, sw, k % FT, :],
                                             start=(k == 0 and sh == 0 and sw == 0),
                                             stop=(k == 2 * FT - 1 and sh == 1))
                    ins.then_inc(down_done, 1)
            eng.wait_ge(xfT_ready, NT + 1)
            up(0, FG, first=True)
            eng.wait_ge(w2_ready, 1)
            with eng.Fori(0, (FGROUPS - 1) // 2) as u:
                up(2 * u + 1, FG)
                down(2 * u, 0, [TN] * 4)
                up(2 * u + 2, FG)
                down(2 * u + 1, 1, [TN] * 4)
            down(FGROUPS - 1, 0, [TN] * 4)

        @block.vector
        def _(eng):
            eng.memset(edge_i[:, 0, ROWS - 1, :], 0)
            eng.memset(edge_i[:, 2, ROWS - 1, :], 0)
            eng.memset(edge_i[:, 1, ROWS - 1, :], int(INVALID)).then_inc(edge_clear, 1)
            eng.memset(small[:, 126:127], 0.0).then_inc(consts_v, 1)
            eng.memset(ones[:, :], 1.0).then_inc(consts_v, 1)
            eng.memset(echk[:, :], 0.0).then_inc(consts_v, 1)
            eng.sem_inc(chunk_mm, MM_CREDIT)
            eng.sem_inc(chunk_add, ADD_CREDIT)
            for s in (self_turned, selfT_ready, lin_done, h_ready, x1_ready, xfT_ready, xf_turned, *gen_mm, *gen_add, *gen_win, *gen_key):
                eng.sem_inc(s, 1)
            for s in (h_out, *o_out):
                eng.sem_inc(s, 16)
            eng.sem_inc(gelu_done, SR)
            eng.sem_inc(y_read, 4)
            eng.sem_inc(tail, TAIL_N)
            eng.sem_inc(low_ready, HR)

            count = [0]

            def step(ins):
                count[0] += 1
                ins.then_inc(pro, 1)
                eng.wait_ge(pro, count[0])

            def bases():
                eng.wait_ge(lists_f, 1)
                eng.tensor_reduce(emin, edge_f[:, 0, :, :], AX.X, ALU.min).then_inc(pro, 1)
                count[0] += 1
                step(eng.tensor_reduce(emax, edge_f[:, 0, :, :], AX.X, ALU.max))
                eng.sem_inc(base_ready, 1)

            eng.wait_ge(consts, 5)
            step(eng.tensor_scalar(ebound_i, ebound_i, GC.bit_length() - 1, None, ALU.arith_shift_right))
            step(eng.tensor_scalar(eupper_i, eupper_i, GC.bit_length() - 1, None, ALU.arith_shift_right))
            step(eng.tensor_scalar(ebound, ebound_i, float(TN), None, ALU.mult))
            step(eng.tensor_scalar(eupper, eupper_i, float(TN), float(AHEAD * TN - WIN), ALU.mult, ALU.add))
            step(eng.tensor_copy(pattern[:, :], pattern_i[:, :]))
            eng.wait_ge(consts_v, 3)

            def stats_of(t):
                return eng.bn_stats(ln_stats[0:TN, t, :], bulk[0:TN, t, :])

            def scale(b, meanwhile=()):
                t0, t1 = XB[b]
                rest = list(meanwhile)

                def step_and(ins):
                    count[0] += 1
                    ins.then_inc(pro, 1)
                    if rest:
                        rest.pop(0)()
                    eng.wait_ge(pro, count[0])
                for t in range(t0, t1):
                    ins = eng.bn_aggr(ln_mv[0:TN, t, :], ln_stats[0:TN, t, :])
                step_and(ins)
                rsqrt_steps(eng, step_and, ln_rs[0:TN, t0:t1], ln_var[0:TN, t0:t1], ln_mv[0:TN, t0:t1, 1],
                            ln_tmp[0:TN, t0:t1])
                assert not rest
                eng.scalar_tensor_tensor(out=ln_shift[0:TN, t0:t1], in0=ln_mv[0:TN, t0:t1, 0], scalar=-1.0,
                                         in1=ln_rs[0:TN, t0:t1], op0=ALU.mult, op1=ALU.mult).then_inc(ln_stat, 1)
            eng.wait_ge(x_in[0], 16)
            for t in range(*XB[0]):
                ins = stats_of(t)
            step(ins)
            for b in range(2):
                eng.wait_ge(x_in[b + 1], 16)
                scale(b, meanwhile=[lambda t=t: stats_of(t).then_inc(ln_stats_in, 1) for t in range(*XB[b + 1])])
                if b == 0:
                    bases()
                eng.wait_ge(ln_stats_in, XB[b + 1][1] - XB[1][0])
            scale(2)
            eng.wait_ge(ln_stat, 3)
            for t in range(XACT, NT):
                ins = eng.tensor_scalar(bulk[0:TN, t, :], bulk[0:TN, t, :], ln_rs[0:TN, t:t + 1],
                                        ln_shift[0:TN, t:t + 1], ALU.mult, ALU.add)
            ins.then_inc(ln_ready_v, 1)
            blocks = [(a, j) for a in range(2) for j in range(ROWS)]
            for n, (a, j) in enumerate(blocks):
                m = P if j < ROWS - 1 else CTAIL
                eng.wait_ge(rows_turned, n + 1)
                to = keyT if a == 0 else idx
                ins = eng.tensor_copy(to[:, j * P:j * P + m], pchunk[n % SR][:, 0:m]).then_inc(turned_out, 1)
            eng.wait_ge(rows_turned, len(blocks) + 2)
            step(eng.tensor_copy(base_row[:, :], plin[0:1, 0:ROWS * P]))
            step(eng.tensor_reduce(r1, ptr[0:1, 0:P], AX.X, ALU.max))
            step(eng.tensor_scalar(order_bad, r1, 0.5, None, ALU.is_gt))
            eng.wait_ge(turned_out, len(blocks))
            eng.sem_inc(edges_ready, 1)
            bad = eng.value_load(order_bad, min_val=0, max_val=1)

            def tile_tail(t, m, part):
                def after(k):
                    eng.wait_ge(tail, TAIL_N * (t + 1) + k)
                if part == 0:
                    eng.wait_ge(lin_done, NT + t + 2)
                    eng.wait_ge(resid_in, 16 * t + 16)
                    eng.tensor_tensor(resid[0:m, :], plin[0:m, 0:D], resid[0:m, :], ALU.add).then_inc(tail, 1)
                elif part == 1:
                    after(1)
                    eng.bn_stats(stats[0:m, :], resid[0:m, :]).then_inc(tail, 1)
                elif part == 2:
                    after(2)
                    eng.sem_inc(passed_v, 1)
                    eng.bn_aggr(mv[0:m, :], stats[0:m, :]).then_inc(tail, 1)
                elif part < 3 + RSQRT_N:
                    after(part)
                    rsqrt_step(eng, part - 3, m).then_inc(tail, 1)
                    if part == 3:
                        eng.tensor_copy(x1_view(t, m), resid[0:m, :].rearrange("p (a b) -> p a b", a=4)).then_inc(x1_ready, 1)
                elif part == 3 + RSQRT_N:
                    after(part)
                    eng.wait_ge(x1_ready, t + 2)
                    eng.wait_ge(xf_turned, t + 1)
                    eng.tensor_scalar(hout[0:m, :].rearrange("p (a b) -> p a b", a=4), x1_view(t, m), mv[0:m, 0:1],
                                      rs[0:m, :], ALU.subtract, ALU.mult).then_inc(tail, 1)
                else:
                    after(part)
                    eng.tensor_copy(xf_view(t, m), hout[0:m, :].rearrange("p (a b) -> p a b", a=4)).then_inc(xf_ready, 1)

            def split_xfT(t, m):
                eng.wait_ge(xf_high, t + 1)
                for h in range(KT):
                    to = xfT[h][:, bass.ds(t, 1), :, 0:m]
                    ins = eng.tensor_tensor(to[:, :, 1, :].rearrange("p a n -> p (a n)"), xft32[:, h, 0:m],
                                            to[:, :, 0, :].rearrange("p a n -> p (a n)"), ALU.subtract)
                ins.then_inc(xfT_ready, 1)

            with eng.If(bad == 0):
                for L in range(2):
                    def one_hot(g, j):
                        eng.tensor_scalar(onehot[j % SR], pattern[:, :], keyT[:, bass.ds(GC * g + j, 1)], None,
                                          ALU.is_equal).then_inc(onehot_ready, 1)

                    def group(g, chunks, clears, end=None):
                        _, base = nc.values_load_multi_w_load_instructions(
                            base_row[0:1, bass.ds(GC * g, GC)], engines=[DVE_ENGINE], min_val=0, max_val=BASE_MAX,
                            skip_runtime_bounds_check_because="a destination node is below N, and a window from there "
                            "ends inside agg")
                        eng.wait_ge(cleared, L * (NT - AHEAD + 1) + clears)
                        part = 0
                        for j in range(chunks):
                            if chunks == GC or j + SR - 1 < chunks:
                                one_hot(g, j + SR - 1)
                            c = L * NCH + GC * g + j
                            eng.wait_ge(chunk_mm, MM_CREDIT + c + 1)
                            eng.wait_ge(chunk_add, ADD_CREDIT + c)
                            to = agg[:, :, :, bass.ds(base[j], WIN)]
                            eng.tensor_tensor(to, to, pchunk[j % SR][:, 0:KT * SC].rearrange(
                                "p (h r n) -> p h r n", h=KT, r=R), ALU.add).then_inc(chunk_add, 1)
                            if L == 1 and end is not None:
                                for _ in range(2):
                                    if part < TAIL_PARTS:
                                        tile_tail(end, TN, part)
                                    part += 1
                                if j == 12:
                                    split_xfT(end, TN)

                    for j in range(SR - 1):
                        one_hot(0, j)
                    group(0, GC, 1)
                    group(1, GC, 2)
                    group(2, GC, 3)
                    with eng.Fori(3, NT - AHEAD) as g:
                        group(g, GC, g + 1, end=g - LAG - 1)
                    for g in range(NT - AHEAD, NG):
                        group(g, GC, NT - AHEAD + 1, end=g - LAG - 1)
                    group(NG, CREST, NT - AHEAD + 1, end=NT - 3)
                    if L == 1:
                        for part in range(TAIL_PARTS):
                            tile_tail(NT - 2, TN, part)
                        for part in range(TAIL_PARTS):
                            tile_tail(NT - 1, TN, part)
                            if part == TAIL_PARTS // 2:
                                split_xfT(NT - 2, TN)
            with eng.Else():
                eng.wait_ge(cleared, 1)
                eng.wait_ge(ln_ready, len(XB))
                eng.wait_ge(ln_ready_v, 1)
                eng.memset(agg[:, :, :, :], 0.0).then_inc(gen_clear, 1)
                eng.wait_ge(gen_clear, 1)
                for L in range(2):
                    def chunk(s, c0, c):
                        eng.wait_ge(gen_key[s], (PASSES + 1) * c + 1)
                        eng.wait_ge(gen_win[s], (PASSES + 1) * c + 1)
                        eng.sem_inc(passed_v, 1)
                        eng.tensor_copy(key_now, keyT[:, bass.ds(c0 + c, 1)]).then_inc(gen_key[s], 1)
                        eng.tensor_copy(base_now, base_row[0:1, bass.ds(c0 + c, 1)]).then_inc(gen_win[s], 1)
                        with eng.Fori(0, PASSES) as k:
                            n = PASSES * c + k
                            eng.wait_ge(gen_key[s], n + c + 2)
                            eng.wait_ge(gen_win[s], n + c + 2)
                            eng.wait_ge(gen_mm[s], n + 1)
                            eng.sem_inc(passed_v, 1)
                            base = eng.value_load(base_now, min_val=0, max_val=BASE_MAX)
                            eng.tensor_scalar(onehot[0], pattern[:, :], key_now, None,
                                              ALU.is_equal).then_inc(gen_hot[s], 1)
                            eng.wait_ge(gen_mm[s], n + 2)
                            eng.wait_ge(gen_add[s], n + 1)
                            to = agg[:, :, :, bass.ds(base, WIN)]
                            eng.tensor_tensor(to, to, pchunk[0][:, 0:KT * SC].rearrange(
                                "p (h r n) -> p h r n", h=KT, r=R), ALU.add).then_inc(gen_add[s], 1)
                            eng.tensor_scalar(key_now, key_now, float(WIN * R), None,
                                              ALU.subtract).then_inc(gen_key[s], 1)
                            eng.tensor_scalar(base_now, base_now, float(WIN), float(BASE_MAX), ALU.add,
                                              ALU.min).then_inc(gen_win[s], 1)
                    general(eng, L, chunk, windows=(gen_key, gen_win))
                    if L == 0:
                        eng.wait_ge(staged, KT * NT)
                        eng.memset(agg[:, :, :, :], 0.0).then_inc(gen_clear, 1)
                        eng.wait_ge(gen_clear, 2)
                    else:
                        def tile(t, m, last):
                            for part in range(TAIL_PARTS):
                                tile_tail(t, m, part)
                            if not last:
                                split_xfT(t, m)
                        with eng.Fori(0, NT - 1) as t:
                            tile(t, TN, False)
                        tile(NT - 1, TN, True)

            n = [0]

            def step(ins):
                n[0] += 1
                ins.then_inc(route, 1)
                eng.wait_ge(route, n[0])

            def mark(want):
                assert n[0] == want, (n[0], want)

            eng.wait_ge(xf_high, NT)
            step(eng.tensor_reduce(sumc, colsum[:, :, :], AX.X, ALU.add))
            mark(ROUTE_SUMS)
            split_xfT(NT - 1, TN)
            eng.wait_ge(ffn_const_in, 48)
            eng.wait_ge(route_pe, 1)
            step(eng.scalar_tensor_tensor(out=lg, in0=pmisc[0:1, 0:NE], scalar=1.0 / N, in1=brow, op0=ALU.mult, op1=ALU.add))
            step(eng.tensor_reduce(r1, lg, AX.X, ALU.max))
            step(eng.tensor_scalar(lg, lg, r1, None, ALU.subtract))
            mark(ROUTE_LOGITS)
            eng.wait_ge(route_act, 1)
            step(eng.reciprocal(r2, rsum))
            step(eng.tensor_scalar(lg, ex, r2, CAPACITY / N, ALU.mult, ALU.min))
            step(eng.tensor_reduce(r1, lg, AX.X, ALU.max))
            step(eng.tensor_scalar(lg, lg, r1, None, ALU.subtract))
            mark(ROUTE_SCALED)
            eng.wait_ge(route_act, 2)
            step(eng.max(top, ex))
            step(eng.max_index(top_i, top, ex))
            mark(ROUTE_TOP)
            step(eng.reciprocal(r2, rsum))
            step(eng.tensor_scalar(lg[:, 0:2], top[:, 0:2], top[:, 0:1], r2, ALU.subtract, ALU.mult))
            mark(ROUTE_DIFF)
            eng.wait_ge(route_act, 3)
            step(eng.reciprocal(r2, rsum))
            step(eng.tensor_scalar(lg[:, 2:4], ex[:, 0:2], r2, None, ALU.mult))
            mark(ROUTE_WEIGHTS)
            eng.wait_ge(route_pe, 2)
            eng.tensor_scalar(wcol, pmisc[:, 0:2], WSCALE, None, ALU.mult).then_inc(wcol_ready, 1)
            for b in range(4):
                e, cols = b // 2, slice(b % 2 * FH, (b % 2 + 1) * FH)
                eng.wait_ge(w1_ready[b], 1)
                eng.scalar_tensor_tensor(out=w1s[:, e, 1, :, cols], in0=w1e[:, e, :, cols], scalar=WSCALE,
                                         in1=w1s[:, e, 0, :, cols], op0=ALU.mult, op1=ALU.subtract).then_inc(w1_ready[b], 1)
                if b == 1:
                    eng.wait_ge(b1_turned, 1)
                    eng.tensor_copy(b1T, ptr[:, 0:2 * FT]).then_inc(b1_ready, 1)
            eng.wait_ge(wcol_ready, 1)
            eng.wait_ge(expert_rest, 16 * 4)
            for e in range(2):
                step(eng.tensor_scalar(w2s[:, e, 0, :, :], w2e[:, e, :, :], wcol[:, e:e + 1], None, ALU.mult))
                step(eng.scalar_tensor_tensor(out=w2s[:, e, 1, :, :], in0=w2e[:, e, :, :], scalar=wcol[:, e:e + 1],
                                              in1=w2s[:, e, 0, :, :], op0=ALU.mult, op1=ALU.subtract))
            eng.sem_inc(w2_ready, 1)
            step(eng.tensor_scalar(b2w, b2rows[:, 0, :], wcol[:, 0:1], None, ALU.mult))
            step(eng.scalar_tensor_tensor(out=b2w, in0=b2rows[:, 1, :], scalar=wcol[:, 1:2], in1=b2w,
                                          op0=ALU.mult, op1=ALU.add))

            def add_bias(t, m):
                eng.scalar_tensor_tensor(out=xf_view(t, m), in0=b2w[0:m, :].rearrange("p (a b) -> p a b", a=4),
                                         scalar=1.0 / WSCALE, in1=xf_view(t, m), op0=ALU.mult,
                                         op1=ALU.add).then_inc(bias_added, 1)
            with eng.Fori(0, NT - 1) as t:
                add_bias(t, TN)
            add_bias(NT - 1, TN)

            ybank = [plin, ptr, pxf, pmisc]

            def finish(q):
                def z(i):
                    return zrow[i][0:TN, :]

                def in_parts(ap):
                    return ap.rearrange("p (a b) -> p a b", a=4)
                y, v, t = (fin_cols[0:TN, k, :] for k in range(3))
                n = [0]

                def step(ins):
                    n[0] += 1
                    ins.then_inc(fin, 1)
                    eng.wait_ge(fin, FIN_N * q + n[0])
                for i in range(4):
                    eng.wait_ge(down_done, 4 * q + i + 1)
                    eng.wait_ge(o_out[i], 16 * q + 16)
                    eng.scalar_tensor_tensor(out=in_parts(z(i)), in0=in_parts(ybank[i][0:TN, 0:D]),
                                             scalar=1.0 / WSCALE, in1=xf_view(4 * q + i, TN), op0=ALU.mult,
                                             op1=ALU.add).then_inc(y_read, 1)
                    eng.wait_ge(y_read, 4 * q + i + 5)
                    ins = eng.bn_stats(fin_stats[0:TN, i, :], z(i))
                step(ins)
                eng.sem_inc(passed_v, 1)
                for i in range(4):
                    ins = eng.bn_aggr(fin_mv[0:TN, i, :], fin_stats[0:TN, i, :])
                step(ins)
                rsqrt_steps(eng, step, y, v, fin_mv[0:TN, :, 1], t)
                for i in range(4):
                    ins = eng.scalar_tensor_tensor(out=z(i), in0=z(i), scalar=fin_mv[0:TN, i, 0:1],
                                                   in1=gam[0:TN, :], op0=ALU.subtract, op1=ALU.mult)
                step(ins)
                for i in range(4):
                    eng.scalar_tensor_tensor(out=in_parts(z(i)), in0=in_parts(z(i)), scalar=y[:, i:i + 1],
                                             in1=x1_view(4 * q + i, TN), op0=ALU.mult, op1=ALU.add).then_inc(o_ready, 1)
                assert n[0] == FIN_N
            FIN_N = 3 + RSQRT_STEPS
            eng.wait_ge(beta_added, NT)
            eng.wait_ge(bias_added, NT)
            with eng.Fori(0, FGROUPS) as q:
                finish(q)


ROUTE_SUMS = 1
ROUTE_LOGITS = 4
ROUTE_SCALED = 8
ROUTE_TOP = 10
ROUTE_DIFF = 12
ROUTE_WEIGHTS = 14


_INS = ["x", "src", "dst", "edge_type_8", "L0_gnn_W1", "L0_gnn_self_w1", "L0_gnn_b1", "L0_gnn_W2", "L0_gnn_self_w2",
        "L0_gnn_b2", "L0_ffn_Wr", "L0_ffn_br", "L0_ffn_W1", "L0_ffn_b1", "L0_ffn_W2", "L0_ffn_b2", "L0_ffn_gamma",
        "L0_ffn_beta"]


def kernel(**inputs):
    import concourse.bacc as bacc
    from concourse.bass_utils import run_bass_kernel_spmd

    nc = bacc.Bacc("TRN2", target_bir_lowering=False, num_devices=1)
    arrays, ap = {}, {}
    for name in _INS:
        a = np.ascontiguousarray(inputs[name])
        arrays["in_" + name] = a
        ap[name] = nc.dram_tensor("in_" + name, a.shape, mybir.dt.from_np(a.dtype), kind="ExternalInput").ap()
    out = nc.dram_tensor("out_rows", (N, D), F32, kind="ExternalOutput").ap()
    program(nc, ap["x"], ap["src"], ap["dst"], ap["edge_type_8"], [ap["L0_gnn_W1"], ap["L0_gnn_W2"]],
            [ap["L0_gnn_self_w1"], ap["L0_gnn_self_w2"]], [ap["L0_gnn_b1"], ap["L0_gnn_b2"]], ap["L0_ffn_Wr"],
            ap["L0_ffn_br"], ap["L0_ffn_W1"], ap["L0_ffn_b1"], ap["L0_ffn_W2"], ap["L0_ffn_b2"], ap["L0_ffn_gamma"],
            ap["L0_ffn_beta"], out)
    result = run_bass_kernel_spmd(nc, [arrays], core_ids=[0])
    return result.results[0]["out_rows"]
```
